# Optimizing a Trainium2 kernel written in Bass

```python
import numpy as np
import jax
import jax.numpy as jnp

def _softmax(x, axis=-1):
    return jax.nn.softmax(x, axis=axis)

def _gelu(x):
    return jax.nn.gelu(x, approximate=True)

def _silu(x):
    return jax.nn.silu(x)

def _sigmoid(x):
    return jax.nn.sigmoid(x)

def _layernorm(x, axis=-1, eps=1e-05):
    m = jnp.mean(x, axis=axis, keepdims=True)
    v = jnp.var(x, axis=axis, keepdims=True)
    return (x - m) / jnp.sqrt(v + eps)

def _scatter_add(tgt, idx, src, axis=0):
    return tgt.at[idx].add(src)

def _segment_sum(src, seg, n):
    return jax.ops.segment_sum(src, seg, n)
kernel_name = 'mk_adaln_ffn_d1_seqx_r8_192d27'

def setup_inputs(seed: int=0):
    np.random.seed(seed)
    _w = jnp.asarray

    def _rec_inputs():
        import jax
        import jax.numpy as jnp
        _rk = jax.random.key(seed)
        x = -7.109e-05 + 0.9999 * jax.random.normal(jax.random.fold_in(_rk, 1), (32, 32, 256), jnp.float32)
        _lenS = 32 - jax.random.randint(jax.random.fold_in(_rk, 7), (32,), 0, max(1, 32 // 4) + 1, jnp.int32)
        _lenS2 = 32 - jax.random.randint(jax.random.fold_in(_rk, 8), (32,), 0, max(1, 32 // 4) + 1, jnp.int32)
        itok_B_1_198 = jax.random.randint(jax.random.fold_in(_rk, 11), (32,), 1, 199, jnp.int32)
        return (x, itok_B_1_198)
    x, itok_B_1_198 = _rec_inputs()

    def _L0_cond_setup():
        import jax, jax.numpy as jnp
        import numpy as np
        B, C, T = (128, 32, 256)
        S, D = (200, 32)
        key = jax.random.key(seed)
        k1, k2, k3 = jax.random.split(key, 3)
        x = jax.random.normal(k1, (B, C, T), dtype=jnp.float32)
        conditions = jax.random.randint(k2, (B,), 0, S, dtype=jnp.int64)
        weights = jax.random.normal(k3, (S, C, D), dtype=jnp.float32) / jnp.sqrt(jnp.float32(C))
        return {'x': x, 'conditions': conditions, 'weights': weights}
    _L0_cond_all = _L0_cond_setup()
    _L0_cond_in = {k: v for k, v in _L0_cond_all.items() if k in ('weights',)}
    del _L0_cond_all

    def _L0_ffn_setup():
        import jax, jax.numpy as jnp
        import numpy as np
        H = 256
        E = 64
        I = 64
        SI = 64
        TOP_K = 8
        B, T = (2, 64)
        key = jax.random.key(seed)
        ks = jax.random.split(key, 8)
        s = 0.02
        return {'h': jax.random.normal(ks[0], (B, T, H), jnp.float32), 'gate_w': jax.random.normal(ks[1], (E, H), jnp.float32) * s, 'gu_w': jax.random.normal(ks[2], (E, 2 * I, H), jnp.float32) * s, 'dp_w': jax.random.normal(ks[3], (E, H, I), jnp.float32) * s, 'sh_gate_w': jax.random.normal(ks[4], (SI, H), jnp.float32) * s, 'sh_up_w': jax.random.normal(ks[5], (SI, H), jnp.float32) * s, 'sh_down_w': jax.random.normal(ks[6], (H, SI), jnp.float32) * s, 'sh_gate1_w': jax.random.normal(ks[7], (1, H), jnp.float32) * s}
    _L0_ffn_all = _L0_ffn_setup()
    _L0_ffn_in = {k: v for k, v in _L0_ffn_all.items() if k in ('gate_w', 'gu_w', 'dp_w', 'sh_gate_w', 'sh_up_w', 'sh_down_w', 'sh_gate1_w')}
    del _L0_ffn_all
    return {'x': x, 'itok_B_1_198': itok_B_1_198, 'L0_cond_weights': _L0_cond_in['weights'], 'L0_ffn_gate_w': _L0_ffn_in['gate_w'], 'L0_ffn_gu_w': _L0_ffn_in['gu_w'], 'L0_ffn_dp_w': _L0_ffn_in['dp_w'], 'L0_ffn_sh_gate_w': _L0_ffn_in['sh_gate_w'], 'L0_ffn_sh_up_w': _L0_ffn_in['sh_up_w'], 'L0_ffn_sh_down_w': _L0_ffn_in['sh_down_w'], 'L0_ffn_sh_gate1_w': _L0_ffn_in['sh_gate1_w']}

def reference(x, itok_B_1_198, L0_cond_weights, L0_ffn_gate_w, L0_ffn_gu_w, L0_ffn_dp_w, L0_ffn_sh_gate_w, L0_ffn_sh_up_w, L0_ffn_sh_down_w, L0_ffn_sh_gate1_w):
    import jax
    import jax.numpy as jnp

    def _L0_cond_ref(x, conditions, weights):
        import jax, jax.numpy as jnp
        import numpy as np
        B, C, T = (128, 32, 256)
        S, D = (200, 32)
        w = weights[conditions]
        return jnp.einsum('bct,bcd->bdt', x, w)

    def _L0_ffn_ref(h, gate_w, gu_w, dp_w, sh_gate_w, sh_up_w, sh_down_w, sh_gate1_w):
        import jax, jax.numpy as jnp
        import numpy as np
        H = 256
        E = 64
        I = 64
        SI = 64
        TOP_K = 8
        B, T = (2, 64)
        Bb, Tt, Hh = h.shape
        x = h.reshape(Bb * Tt, Hh)
        N = x.shape[0]
        logits = x @ gate_w.T
        topv, topi = jax.lax.top_k(logits, TOP_K)
        rw = jax.nn.softmax(topv.astype(jnp.float32), axis=-1).astype(x.dtype)
        W = jnp.zeros((N, E), x.dtype).at[jnp.arange(N)[:, None], topi].set(rw)
        gu = jnp.einsum('nh,eih->nei', x, gu_w)
        gate, up = (gu[..., :I], gu[..., I:])
        inter = jax.nn.silu(gate) * up
        inter_w = inter * W[:, :, None]
        out = jnp.einsum('nei,ehi->nh', inter_w, dp_w)
        sh_inter = jax.nn.silu(x @ sh_gate_w.T) * (x @ sh_up_w.T)
        sh_out = sh_inter @ sh_down_w.T
        sh_g = jax.nn.sigmoid(x @ sh_gate1_w.T)
        out = out + sh_g * sh_out
        return out.reshape(Bb, Tt, Hh)
    x = x + _L0_ffn_ref(_L0_cond_ref(x, itok_B_1_198, L0_cond_weights), L0_ffn_gate_w, L0_ffn_gu_w, L0_ffn_dp_w, L0_ffn_sh_gate_w, L0_ffn_sh_up_w, L0_ffn_sh_down_w, L0_ffn_sh_gate1_w)
    return x

_drawn_inputs = setup_inputs


def setup_inputs(seed=0):
    import zlib

    import numpy as np

    out = dict(_drawn_inputs(seed))
    spreads = {}
    factors = {'L0_cond_weights': 8.0,
     'L0_ffn_gate_w': 8.0,
     'L0_ffn_gu_w': 8.0,
     'L0_ffn_dp_w': 8.0,
     'L0_ffn_sh_gate_w': 8.0,
     'L0_ffn_sh_up_w': 8.0,
     'L0_ffn_sh_down_w': 8.0,
     'L0_ffn_sh_gate1_w': 8.0}
    for name, (base, spread) in spreads.items():
        noise = np.random.default_rng([zlib.crc32(name.encode()), seed]).standard_normal(out[name].shape)
        drawn = base * np.exp(spread * noise) if base else spread * noise
        out[name] = jnp.asarray(drawn.astype(out[name].dtype))
    for name, factor in factors.items():
        out[name] = (out[name] * factor).astype(out[name].dtype)
    return out
```

```python
from contextlib import ExitStack

import concourse.bass as bass
from concourse import mybir

BATCH, CHAN, TIME = 32, 32, 256
STATES, COND = 200, 32
TOKENS = BATCH * COND
HALF = TOKENS // 2
KC = TIME // 128
EXPERTS, INNER, TOP = 64, 64, 8
PAIRS = EXPERTS // 2
LOGITS = EXPERTS + 2
BLOCKS = TOKENS // 128
GROUPS = BATCH * CHAN // 128
LAG = 3
SLOTS = 4
UNITS = 2 * PAIRS


def adaln_moe_kernel(nc, x, x_t, itok, cond_w, router_w, gu_w, dp_w, out_t):
    f32, f32r, i32 = mybir.dt.float32, mybir.dt.float32r, mybir.dt.int32
    ALU = mybir.AluOpType
    ACT = mybir.ActivationFunctionType
    AX = mybir.AxisListType

    routing_dram = nc.dram_tensor("routing_dram", (EXPERTS + 1, TOKENS), f32, kind="Internal").ap()

    ctx = ExitStack()
    with ctx:
        def sb(name, shape, dt=f32):
            return ctx.enter_context(nc.sbuf_tensor(name, shape, dt))

        def ps(name, shape, dt=f32):
            return ctx.enter_context(nc.psum_tensor(name, shape, dt))

        def sem(name):
            return ctx.enter_context(nc.semaphore(name))

        x_sb = sb("x_sb", [128, GROUPS, TIME])
        itok_sb = sb("itok_sb", [128, GROUPS], i32)
        chan_of_row = sb("chan_of_row", [128, 1])
        clamped = sb("clamped", [128, GROUPS])
        table_row = sb("table_row", [128, GROUPS], i32)
        gathered = sb("gathered", [128, GROUPS, COND])
        diag = sb("diag", [128, GROUPS, 128])
        h_hi = sb("h_hi", [128, KC, TOKENS], f32r)
        h_lo = sb("h_lo", [128, KC, TOKENS], f32r)
        rw_raw = sb("rw_raw", [128, KC, LOGITS])
        rw_hi = sb("rw_hi", [128, KC, LOGITS], f32r)
        rw_lo = sb("rw_lo", [128, KC, LOGITS], f32r)
        top8 = sb("top8", [128, BLOCKS, TOP])
        shifted = sb("shifted", [128, BLOCKS, 2, EXPERTS])
        small = sb("small", [128, BLOCKS * TOP + BLOCKS])
        denom = sb("denom", [128, 2 * BLOCKS])
        recip = sb("recip", [128, 2 * BLOCKS])
        route = sb("route", [128, BLOCKS, EXPERTS + 1])
        route_t = sb("route_t", [EXPERTS + 1, TOKENS])
        ident = sb("ident", [128, 128])
        gu_raw = sb("gu_raw", [128, 2, KC * 256])
        gu_hi = sb("gu_hi", [128, 2, KC * 256], f32r)
        gu_lo = sb("gu_lo", [128, 2, KC * 256], f32r)
        dp_raw = sb("dp_raw", [128, 2, TIME])
        dp_hi = sb("dp_hi", [128, 2, TIME], f32r)
        dp_lo = sb("dp_lo", [128, 2, TIME], f32r)
        route_bc = sb("route_bc", [128, 2, TOKENS])
        silu_sb = sb("silu_sb", [128, 2, HALF])
        inter = sb("inter", [128, SLOTS, HALF])
        inter_hi = sb("inter_hi", [128, SLOTS, HALF], f32r)
        inter_lo = sb("inter_lo", [128, SLOTS, HALF], f32r)
        xt_sb = sb("xt_sb", [128, KC, TOKENS])
        out_sb = sb("out_sb", [128, KC, TOKENS])

        acc = ps("acc", [128, KC * 2, HALF])
        gate_ps = ps("gate_ps", [128, 2, HALF])
        up_ps = ps("up_ps", [128, 2, HALF])

        itok_in = sem("itok_in")
        x_in = sem("x_in")
        rw_in = sem("rw_in")
        xt_in = sem("xt_in")
        gu_in = [sem(f"gu_in{s}") for s in range(2)]
        dp_in = [sem(f"dp_in{s}") for s in range(2)]
        route_in = [sem(f"route_in{s}") for s in range(2)]
        chan_ready = sem("chan_ready")
        clamp_done = sem("clamp_done")
        table_row_ready = sem("table_row_ready")
        gather_in = sem("gather_in")
        diag_zero = sem("diag_zero")
        diag_ready = sem("diag_ready")
        ident_step = sem("ident_step")
        h_ps_ready = sem("h_ps_ready")
        h_hi_ready = sem("h_hi_ready")
        h_ready = sem("h_ready")
        rw_hi_ready = sem("rw_hi_ready")
        rw_ready = sem("rw_ready")
        logits_ready = sem("logits_ready")
        router_step = sem("router_step")
        shifted_ready = sem("shifted_ready")
        exp_ready = sem("exp_ready")
        route_ready = sem("route_ready")
        route_t_ps_ready = sem("route_t_ps_ready")
        route_t_ready = sem("route_t_ready")
        route_out = sem("route_out")
        gu_hi_ready = sem("gu_hi_ready")
        gu_ready = sem("gu_ready")
        dp_hi_ready = sem("dp_hi_ready")
        dp_ready = sem("dp_ready")
        gate_done = sem("gate_done")
        up_done = sem("up_done")
        silu_done = sem("silu_done")
        gated = sem("gated")
        weighted = sem("weighted")
        inter_hi_ready = sem("inter_hi_ready")
        inter_ready = sem("inter_ready")
        down_done = sem("down_done")
        acc_done = sem("acc_done")
        out_ready = sem("out_ready")
        stored = sem("stored")

        block = ctx.enter_context(nc.Block())

        @block.sync
        def _(sp):
            for j in range(4):
                sp.dma_start(itok_sb[32 * j:32 * j + 32, :],
                             itok[j:j + 1, :].to_broadcast([32, GROUPS])
                             ).then_inc(itok_in, 16)
            sp.dma_start(x_sb[:, :, :], x.rearrange("(g p) t -> p g t", p=128)).then_inc(x_in, 16)
            sp.dma_start(rw_raw[:, :, :], router_w.rearrange("(k p) e -> p k e", p=128)).then_inc(rw_in, 16)
            for p in range(2):
                sp.dma_start(gu_raw[:, p, :], gu_w[p, :, :]).then_inc(gu_in[p], 16)
                sp.dma_start(dp_raw[:, p, :], dp_w[p, :, :]).then_inc(dp_in[p], 16)
            sp.dma_start(xt_sb[:, :, :], x_t.rearrange("(k p) n -> p k n", p=128)).then_inc(xt_in, 16)

            sp.wait_ge(route_t_ready, 2)
            sp.dma_start(routing_dram, route_t[:, :]).then_inc(route_out, 16)
            sp.wait_ge(route_out, 16)

            def load_route(p, s):
                for e in range(2):
                    sp.dma_start(route_bc[64 * e:64 * e + 64, s, :],
                                 routing_dram[bass.ds(p * 2 + e, 1), :].to_broadcast([64, TOKENS])
                                 ).then_inc(route_in[s], 16)

            for p in range(2):
                load_route(p, p)
            with sp.Fori(0, PAIRS // 2 - 1) as i:
                for s in range(2):
                    sp.wait_ge(gu_ready, i * 2 + (s + 1))
                    sp.dma_start(gu_raw[:, s, :], gu_w[bass.ds(i * 2 + (s + 2), 1), :, :]
                                 .rearrange("a p n -> (a p) n")).then_inc(gu_in[s], 16)
                    sp.wait_ge(dp_ready, i * 2 + (s + 1))
                    sp.dma_start(dp_raw[:, s, :], dp_w[bass.ds(i * 2 + (s + 2), 1), :, :]
                                 .rearrange("a p n -> (a p) n")).then_inc(dp_in[s], 16)
                    sp.wait_ge(weighted, i * 4 + (2 * s + 2))
                    load_route(i * 2 + (s + 2), s)
            sp.wait_ge(gu_ready, PAIRS - 1)
            sp.dma_start(gu_raw[:, 0, :], gu_w[PAIRS, :, :]).then_inc(gu_in[0], 16)
            sp.wait_ge(dp_ready, PAIRS - 1)
            sp.dma_start(dp_raw[:, 0, :], dp_w[PAIRS, :, :]).then_inc(dp_in[0], 16)
            sp.wait_ge(weighted, UNITS - 2)
            sp.dma_start(route_bc[0:64, 0, :], routing_dram[EXPERTS:EXPERTS + 1, :].to_broadcast([64, TOKENS])
                         ).then_inc(route_in[0], 16)
            for n, (half, k) in enumerate([(0, 0), (0, 1), (1, 0), (1, 1)]):
                sp.wait_ge(out_ready, n + 1)
                sp.dma_start(out_t[k * 128:k * 128 + 128, half * HALF:(half + 1) * HALF],
                             out_sb[:, k, half * HALF:(half + 1) * HALF]).then_inc(stored, 16)
            sp.wait_ge(stored, 64)

        @block.gpsimd
        def _(pool):
            for j in range(4):
                pool.iota(chan_of_row[32 * j:32 * j + 32, :], pattern=[[0, 1]], base=0, channel_multiplier=1,
                          allow_small_or_imprecise_dtypes=True).then_inc(chan_ready, 1)
            pool.wait_ge(table_row_ready, 1)
            for g in range(GROUPS):
                pool.indirect_dma_start(
                    out=gathered[:, g, :], out_offset=None, in_=cond_w,
                    in_offset=bass.IndirectOffsetOnAxis(ap=table_row[:, g:g + 1], axis=0),
                    bounds_check=STATES * CHAN - 1, oob_is_err=False).then_inc(gather_in, 16)
            pool.memset(ident[:, :], 0.0).then_inc(ident_step, 1)
            pool.wait_ge(ident_step, 1)
            pool.affine_select(out=ident[:, :], in_=ident[:, :], compare_op=ALU.not_equal, fill=1.0,
                               base=0, pattern=[[-1, 128]], channel_multiplier=1).then_inc(ident_step, 1)

            def weight(i, j):
                s, half = j // 2, j % 2
                pool.wait_ge(gated, i * 4 + (j + 1))
                if half == 0:
                    pool.wait_ge(route_in[s], i * 32 + 32)
                pool.tensor_tensor(inter[:, j, :], inter[:, j, :],
                                   route_bc[:, s, half * HALF:(half + 1) * HALF], ALU.mult
                                   ).then_inc(weighted, 1)

            with pool.Fori(0, PAIRS // 2) as i:
                for j in range(SLOTS):
                    weight(i, j)
            pool.wait_ge(route_in[0], 16 * PAIRS + 16)
            for half in range(2):
                pool.wait_ge(gated, UNITS + half + 1)
                pool.tensor_tensor(inter[0:64, half, :], inter[0:64, half, :],
                                   route_bc[0:64, 0, half * HALF:(half + 1) * HALF], ALU.mult
                                   ).then_inc(weighted, 1)

        @block.scalar
        def _(act):
            act.wait_ge(rw_in, 16)
            act.activation(rw_hi[:, :, :], rw_raw[:, :, :], ACT.Copy).then_inc(rw_hi_ready, 1)

            def split_gu(i, s, first):
                act.wait_ge(gu_in[s], i * 16 + 16)
                if not first:
                    act.wait_ge(up_done, i * 4 + (2 * s - 2))
                act.activation(gu_hi[:, s, :], gu_raw[:, s, :], ACT.Copy).then_inc(gu_hi_ready, 1)

            def split_dp(i, s, first):
                act.wait_ge(dp_in[s], i * 16 + 16)
                if not first:
                    act.wait_ge(down_done, i * 4 + (2 * s - 2))
                act.activation(dp_hi[:, s, :], dp_raw[:, s, :], ACT.Copy).then_inc(dp_hi_ready, 1)

            def silu(i, j, first):
                act.wait_ge(gate_done, i * 4 + (j + 1))
                if not (first and j < 2):
                    act.wait_ge(gated, i * 4 + (j - 1))
                act.activation(silu_sb[:, j % 2, :], gate_ps[:, j % 2, :], ACT.Silu).then_inc(silu_done, 1)

            def inter_split(i, j, first):
                act.wait_ge(weighted, i * 4 + (j + 1))
                if not first:
                    act.wait_ge(down_done, i * 4 + (j - 3))
                act.activation(inter_hi[:, j % SLOTS, :], inter[:, j % SLOTS, :], ACT.Copy
                               ).then_inc(inter_hi_ready, 1)

            split_gu(0, 0, True)
            for n, (half, k) in enumerate([(0, 0), (0, 1), (1, 0), (1, 1)]):
                act.wait_ge(h_ps_ready, n + 1)
                act.activation(h_hi[:, k, half * HALF:(half + 1) * HALF], acc[:, 2 * k + half, :], ACT.Copy
                               ).then_inc(h_hi_ready, 1)
            silu(0, 0, True)
            act.wait_ge(shifted_ready, 2)
            act.activation(small[:, :], small[:, :], ACT.Exp).then_inc(exp_ready, 1)
            act.activation(shifted[:, :, :, :], shifted[:, :, :, :], ACT.Exp).then_inc(exp_ready, 1)
            split_gu(0, 1, True)
            silu(0, 1, True)
            split_dp(0, 0, True)
            silu(0, 2, True)
            silu(0, 3, True)
            split_gu(1, 0, False)
            for j in range(3):
                inter_split(0, j, True)
            split_dp(0, 1, True)
            with act.Fori(1, PAIRS // 2) as i:
                for j in range(SLOTS):
                    silu(i, j, False)
                    if j == 0:
                        inter_split(i - 1, 3, False)
                        split_gu(i, 1, False)
                    if j == 1:
                        inter_split(i, 0, False)
                        split_dp(i, 0, False)
                    if j == 2:
                        inter_split(i, 1, False)
                        split_gu(i + 1, 0, False)
                    if j == 3:
                        inter_split(i, 2, False)
                        split_dp(i, 1, False)
            last = PAIRS // 2
            inter_split(last - 1, 3, False)
            for half in range(2):
                act.wait_ge(gate_done, UNITS + half + 1)
                act.wait_ge(gated, UNITS + half - 1)
                act.activation(silu_sb[0:64, half, :], gate_ps[0:64, half, :], ACT.Silu).then_inc(silu_done, 1)
                if half == 0:
                    split_dp(last, 0, False)
            for half in range(2):
                act.wait_ge(weighted, UNITS + half + 1)
                act.wait_ge(down_done, UNITS + half - 3)
                act.activation(inter_hi[0:64, half, :], inter[0:64, half, :], ACT.Copy).then_inc(inter_hi_ready, 1)

        @block.vector
        def _(dve):
            dve.memset(diag[:, :, :], 0.0).then_inc(diag_zero, 1)
            dve.wait_ge(itok_in, 64)
            dve.tensor_scalar(clamped[:, :], itok_sb[:, :], 0.0, float(STATES - 1), ALU.max, ALU.min
                              ).then_inc(clamp_done, 1)
            dve.wait_ge(clamp_done, 1)
            dve.wait_ge(chan_ready, 4)
            dve.tensor_scalar(table_row[:, :], clamped[:, :], float(CHAN), chan_of_row[:, 0:1], ALU.mult, ALU.add
                              ).then_inc(table_row_ready, 1)
            dve.wait_ge(rw_hi_ready, 1)
            dve.tensor_tensor(rw_lo[:, :, :], rw_raw[:, :, :], rw_hi[:, :, :].bitcast(f32), ALU.subtract
                              ).then_inc(rw_ready, 1)
            dve.wait_ge(diag_zero, 1)
            dve.wait_ge(gather_in, 16 * GROUPS)
            for j in range(4):
                r = slice(32 * j, 32 * j + 32)
                dve.tensor_copy(diag[r, :, 32 * j:32 * j + 32], gathered[r, :, :]).then_inc(diag_ready, 1)

            def split_gu(i, s):
                dve.wait_ge(gu_hi_ready, i * 2 + (s + 1))
                dve.tensor_tensor(gu_lo[:, s, :], gu_raw[:, s, :], gu_hi[:, s, :].bitcast(f32), ALU.subtract
                                  ).then_inc(gu_ready, 1)

            def split_dp(i, s):
                dve.wait_ge(dp_hi_ready, i * 2 + (s + 1))
                dve.tensor_tensor(dp_lo[:, s, :], dp_raw[:, s, :], dp_hi[:, s, :].bitcast(f32), ALU.subtract
                                  ).then_inc(dp_ready, 1)

            def gate(i, j, first):
                dve.wait_ge(silu_done, i * 4 + (j + 1))
                dve.wait_ge(up_done, i * 4 + (j + 1))
                if not first:
                    dve.wait_ge(inter_ready, i * 4 + (j - 3))
                dve.tensor_tensor(inter[:, j, :], silu_sb[:, j % 2, :], up_ps[:, j % 2, :], ALU.mult
                                  ).then_inc(gated, 1)

            def inter_split(i, j):
                dve.wait_ge(inter_hi_ready, i * 4 + (j + 1))
                dve.tensor_tensor(inter_lo[:, j, :], inter[:, j, :], inter_hi[:, j, :].bitcast(f32), ALU.subtract
                                  ).then_inc(inter_ready, 1)

            split_gu(0, 0)
            for n, (half, k) in enumerate([(0, 0), (0, 1), (1, 0), (1, 1)]):
                dve.wait_ge(h_hi_ready, n + 1)
                hs = slice(half * HALF, (half + 1) * HALF)
                dve.tensor_tensor(h_lo[:, k, hs], acc[:, 2 * k + half, :], h_hi[:, k, hs].bitcast(f32),
                                  ALU.subtract).then_inc(h_ready, 1)

            steps = 0
            bank = [acc[:, half, 0:4 * LOGITS].rearrange("p (b e) -> p b e", b=4) for half in range(2)]
            for half in range(2):
                dve.wait_ge(logits_ready, half + 1)
                for b in range(4):
                    steps += 1
                    dve.max(top8[:, 4 * half + b, :], bank[half][:, b, 0:EXPERTS]).then_inc(router_step, 1)
            for half in range(2):
                dve.wait_ge(router_step, 4 * half + 4)
                for b in range(4):
                    steps += 1
                    dve.match_replace(shifted[:, 4 * half + b, 1, :], top8[:, 4 * half + b, :],
                                      bank[half][:, b, 0:EXPERTS], -3.0e38).then_inc(router_step, 1)
            for half in range(2):
                b4 = slice(4 * half, 4 * half + 4)
                steps += 1
                dve.tensor_tensor(shifted[:, b4, 0, :], bank[half][:, :, 0:EXPERTS],
                                  top8[:, b4, 0:1].to_broadcast([128, 4, EXPERTS]), ALU.subtract
                                  ).then_inc(router_step, 1)
                steps += 1
                dve.tensor_scalar(small[:, BLOCKS * TOP + 4 * half:BLOCKS * TOP + 4 * half + 4],
                                  bank[half][:, :, EXPERTS], -1.0, None, ALU.mult).then_inc(router_step, 1)
            steps += 1
            dve.tensor_tensor(small[:, 0:BLOCKS * TOP].rearrange("p (b e) -> p b e", b=BLOCKS), top8[:, :, :],
                              top8[:, :, 0:1].to_broadcast([128, BLOCKS, TOP]), ALU.subtract
                              ).then_inc(router_step, 1)
            dve.wait_ge(router_step, steps)
            dve.tensor_tensor(shifted[:, :, 1, :], shifted[:, :, 1, :],
                              top8[:, :, 0:1].to_broadcast([128, BLOCKS, EXPERTS]), ALU.subtract
                              ).then_inc(shifted_ready, 2)
            gate(0, 0, True)
            dve.wait_ge(exp_ready, 1)
            dve.tensor_reduce(denom[:, 0:BLOCKS], small[:, 0:BLOCKS * TOP].rearrange("p (b e) -> p b e", b=BLOCKS),
                              AX.X, ALU.add).then_inc(router_step, 1)
            dve.tensor_scalar(denom[:, BLOCKS:2 * BLOCKS], small[:, BLOCKS * TOP:BLOCKS * TOP + BLOCKS], 1.0, None,
                              ALU.add).then_inc(router_step, 1)
            dve.wait_ge(router_step, steps + 2)
            dve.reciprocal(recip[:, :], denom[:, :]).then_inc(router_step, 1)
            dve.wait_ge(exp_ready, 2)
            dve.tensor_tensor(route[:, :, 0:EXPERTS], shifted[:, :, 0, :], shifted[:, :, 1, :], ALU.subtract
                              ).then_inc(router_step, 1)
            dve.wait_ge(router_step, steps + 4)
            dve.tensor_copy(route[:, :, EXPERTS], recip[:, BLOCKS:2 * BLOCKS]).then_inc(route_ready, 1)
            dve.tensor_tensor(route[:, :, 0:EXPERTS], route[:, :, 0:EXPERTS],
                              recip[:, 0:BLOCKS].rearrange("p (b e) -> p b e", e=1)
                              .to_broadcast([128, BLOCKS, EXPERTS]), ALU.mult).then_inc(route_ready, 1)
            split_gu(0, 1)
            gate(0, 1, True)
            for half in range(2):
                dve.wait_ge(route_t_ps_ready, half + 1)
                dve.tensor_copy(route_t[:, half * HALF:(half + 1) * HALF], acc[0:EXPERTS + 1, 2 + half, :]
                                ).then_inc(route_t_ready, 1)
            split_dp(0, 0)
            gate(0, 2, True)
            gate(0, 3, True)
            split_gu(1, 0)
            for j in range(3):
                inter_split(0, j)
            split_dp(0, 1)
            with dve.Fori(1, PAIRS // 2) as i:
                for j in range(SLOTS):
                    gate(i, j, False)
                    if j == 0:
                        inter_split(i - 1, 3)
                        split_gu(i, 1)
                    if j == 1:
                        inter_split(i, 0)
                        split_dp(i, 0)
                    if j == 2:
                        inter_split(i, 1)
                        split_gu(i + 1, 0)
                    if j == 3:
                        inter_split(i, 2)
                        split_dp(i, 1)
            last = PAIRS // 2
            inter_split(last - 1, 3)
            for half in range(2):
                dve.wait_ge(silu_done, UNITS + half + 1)
                dve.wait_ge(inter_ready, UNITS + half - 3)
                dve.tensor_tensor(inter[0:64, half, :], silu_sb[0:64, half, :], gate_ps[64:128, half, :], ALU.mult
                                  ).then_inc(gated, 1)
                if half == 0:
                    split_dp(last, 0)
            for half in range(2):
                dve.wait_ge(inter_hi_ready, UNITS + half + 1)
                dve.tensor_tensor(inter_lo[0:64, half, :], inter[0:64, half, :],
                                  inter_hi[0:64, half, :].bitcast(f32), ALU.subtract).then_inc(inter_ready, 1)
            dve.wait_ge(xt_in, 16)
            for n, (half, k) in enumerate([(0, 0), (0, 1), (1, 0), (1, 1)]):
                hs = slice(half * HALF, (half + 1) * HALF)
                dve.wait_ge(acc_done, n + 1)
                dve.tensor_tensor(out_sb[:, k, hs], acc[:, 2 * k + half, :], xt_sb[:, k, hs], ALU.add
                                  ).then_inc(out_ready, 1)

        @block.tensor
        def _(pe):
            def passes(out, w_hi, w_lo, m_hi, m_lo, start, stop):
                pe.matmul(out, w_hi, m_hi, start=start, stop=False)
                pe.matmul(out, w_hi, m_lo, start=False, stop=False)
                return pe.matmul(out, w_lo, m_hi, start=False, stop=stop)

            pe.wait_ge(x_in, 16)
            pe.wait_ge(diag_ready, 4)
            for half in range(2):
                for k in range(KC):
                    for g in range(GROUPS // 2):
                        gg = half * (GROUPS // 2) + g
                        mm = pe.matmul(acc[:, 2 * k + half, g * 128:g * 128 + 128],
                                       x_sb[:, gg, k * 128:k * 128 + 128], diag[:, gg, :], start=True, stop=True)
                    mm.then_inc(h_ps_ready, 1)
            pe.wait_ge(rw_ready, 1)
            for half in range(2):
                pe.wait_ge(h_ready, 2 * half + 2)
                for b in range(4):
                    n = slice((4 * half + b) * 128, (4 * half + b + 1) * 128)
                    for k in range(KC):
                        mm = passes(acc[:, half, b * LOGITS:(b + 1) * LOGITS], h_hi[:, k, n], h_lo[:, k, n],
                                    rw_hi[:, k, :], rw_lo[:, k, :], k == 0, k == KC - 1)
                mm.then_inc(logits_ready, 1)

            def gate_up(i, j, first):
                s, half = j // 2, j % 2
                if half == 0:
                    pe.wait_ge(gu_ready, i * 2 + (s + 1))
                if not (first and j < 2):
                    pe.wait_ge(gated, i * 4 + (j - 1))
                for part, bank, done in ((0, gate_ps, gate_done), (128, up_ps, up_done)):
                    for k in range(KC):
                        w = slice(k * 256 + part, k * 256 + part + 128)
                        n = slice(half * HALF, (half + 1) * HALF)
                        mm = passes(bank[:, half, :], gu_hi[:, s, w], gu_lo[:, s, w], h_hi[:, k, n], h_lo[:, k, n],
                                    k == 0, k == KC - 1)
                    mm.then_inc(done, 1)

            def down(i, j, first):
                s, half = j // 2, j % 2
                if half == 0:
                    pe.wait_ge(dp_ready, i * 2 + (s + 1))
                pe.wait_ge(inter_ready, i * 4 + (j + 1))
                for k in range(KC):
                    w = slice(k * 128, k * 128 + 128)
                    mm = passes(acc[:, 2 * k + half, :], dp_hi[:, s, w], dp_lo[:, s, w],
                                inter_hi[:, j, :], inter_lo[:, j, :], first and s == 0, False)
                mm.then_inc(down_done, 1)

            pe.wait_ge(h_ready, 4)
            for j in range(3):
                gate_up(0, j, True)
            pe.wait_ge(ident_step, 2)
            pe.wait_ge(route_ready, 2)
            for half in range(2):
                for b in range(4):
                    mm = pe.transpose(acc[0:EXPERTS + 1, 2 + half, b * 128:b * 128 + 128],
                                      route[:, 4 * half + b, :], ident[:, :])
                mm.then_inc(route_t_ps_ready, 1)
            gate_up(0, 3, True)
            down(0, 0, True)
            first = True
            for j in (0, 1, 2, 3):
                gate_up(1, j, False)
                down(0 if j < 3 else 1, (j + 1) % 4, first and j < 3)
            with pe.Fori(2, PAIRS // 2) as i:
                for j in range(SLOTS):
                    gate_up(i, j, False)
                    down(i - 1 if j < 3 else i, (j + 1) % 4, False)
            last = PAIRS // 2
            pe.wait_ge(gu_ready, PAIRS + 1)
            for half in range(2):
                pe.wait_ge(gated, UNITS + half - 1)
                for k in range(KC):
                    w = slice(k * 256, k * 256 + 128)
                    n = slice(half * HALF, (half + 1) * HALF)
                    mm = passes(gate_ps[:, half, :], gu_hi[:, 0, w], gu_lo[:, 0, w], h_hi[:, k, n], h_lo[:, k, n],
                                k == 0, k == KC - 1)
                mm.then_inc(gate_done, 1)
                down(last - 1, half + 1, False)
            down(last - 1, 3, False)
            pe.wait_ge(dp_ready, PAIRS + 1)
            for half in range(2):
                pe.wait_ge(inter_ready, UNITS + half + 1)
                for k in range(KC):
                    w = slice(k * 128, k * 128 + 128)
                    passes(acc[:, 2 * k + half, :], dp_hi[0:64, 0, w], dp_lo[0:64, 0, w],
                           inter_hi[0:64, half, :], inter_lo[0:64, half, :], False, True).then_inc(acc_done, 1)


def kernel(x, itok_B_1_198, L0_cond_weights, L0_ffn_gate_w, L0_ffn_gu_w, L0_ffn_dp_w, L0_ffn_sh_gate_w,
           L0_ffn_sh_up_w, L0_ffn_sh_down_w, L0_ffn_sh_gate1_w):
    import numpy as np
    import concourse.bacc as bacc
    from concourse.bass_utils import run_bass_kernel_spmd

    x, gu, dp = np.asarray(x), np.asarray(L0_ffn_gu_w), np.asarray(L0_ffn_dp_w)
    sh_gate, sh_up, sh_down = map(np.asarray, (L0_ffn_sh_gate_w, L0_ffn_sh_up_w, L0_ffn_sh_down_w))
    f32 = gu.dtype

    gu_all = np.zeros((PAIRS + 1, 128, KC, 2, 128), f32)
    gu_all[:PAIRS] = gu.reshape(PAIRS, 2, 2, INNER, KC, 128).transpose(0, 5, 4, 2, 1, 3).reshape(
        PAIRS, 128, KC, 2, 128)
    gu_all[PAIRS, :, :, 0, :INNER] = sh_gate.reshape(INNER, KC, 128).transpose(2, 1, 0)
    gu_all[PAIRS, :, :, 0, INNER:] = sh_up.reshape(INNER, KC, 128).transpose(2, 1, 0)
    dp_all = np.zeros((PAIRS + 1, 128, TIME), f32)
    dp_all[:PAIRS] = dp.reshape(PAIRS, 2, TIME, INNER).transpose(0, 1, 3, 2).reshape(PAIRS, 128, TIME)
    dp_all[PAIRS, :INNER] = sh_down.T
    router = np.zeros((TIME, LOGITS), f32)
    router[:, :EXPERTS] = np.asarray(L0_ffn_gate_w).T
    router[:, EXPERTS] = np.asarray(L0_ffn_sh_gate1_w)[0]

    arrays = {
        "x": np.ascontiguousarray(x.reshape(BATCH * CHAN, TIME)),
        "x_t": np.ascontiguousarray(x.reshape(TOKENS, TIME).T),
        "itok": np.ascontiguousarray(np.asarray(itok_B_1_198).reshape(GROUPS, 4).T),
        "cond_w": np.ascontiguousarray(np.asarray(L0_cond_weights).reshape(STATES * CHAN, COND)),
        "router_w": router,
        "gu_w": gu_all.reshape(PAIRS + 1, 128, KC * 256),
        "dp_w": dp_all,
    }
    nc = bacc.Bacc("TRN2", target_bir_lowering=False, num_devices=1)
    args = [nc.dram_tensor(f"in_{n}", a.shape, mybir.dt.from_np(a.dtype), kind="ExternalInput").ap()
            for n, a in arrays.items()]
    out = nc.dram_tensor("out_t", (TIME, TOKENS), mybir.dt.from_np(x.dtype), kind="ExternalOutput").ap()
    adaln_moe_kernel(nc, *args, out)
    r = run_bass_kernel_spmd(nc, [{f"in_{n}": a for n, a in arrays.items()}], core_ids=[0])
    return np.ascontiguousarray(r.results[0]["out_t"].T).reshape(x.shape)
```

```python
from contextlib import ExitStack

import concourse.bass as bass
from concourse import mybir

BATCH, CHAN, TIME = 32, 32, 256
STATES, COND = 200, 32
TOKENS = BATCH * COND
HALF = TOKENS // 2
KC = TIME // 128
EXPERTS, INNER, TOP = 64, 64, 8
PAIRS = EXPERTS // 2
LOGITS = EXPERTS + 2
BLOCKS = TOKENS // 128
GROUPS = BATCH * CHAN // 128
SLOTS = 4
WARM_UP = 24
UNITS = 2 * PAIRS


def adaln_moe_kernel(nc, x, x_t, itok, cond_w, router_w, gu_w, dp_w, out_t):
    f32, f32r, i32 = mybir.dt.float32, mybir.dt.float32r, mybir.dt.int32
    ALU = mybir.AluOpType
    ACT = mybir.ActivationFunctionType
    AX = mybir.AxisListType

    routing_dram = nc.dram_tensor("routing_dram", (EXPERTS + 1, TOKENS), f32, kind="Internal").ap()

    ctx = ExitStack()
    with ctx:
        def sb(name, shape, dt=f32):
            return ctx.enter_context(nc.sbuf_tensor(name, shape, dt))

        def ps(name, shape, dt=f32):
            return ctx.enter_context(nc.psum_tensor(name, shape, dt))

        def sem(name):
            return ctx.enter_context(nc.semaphore(name))

        x_sb = sb("x_sb", [128, GROUPS, TIME])
        itok_sb = sb("itok_sb", [128, GROUPS], i32)
        chan_of_row = sb("chan_of_row", [128, 1])
        clamped = sb("clamped", [128, GROUPS])
        table_row = sb("table_row", [128, GROUPS], i32)
        gathered = sb("gathered", [128, GROUPS, COND])
        diag = sb("diag", [128, GROUPS, 128])
        h_hi = sb("h_hi", [128, KC, TOKENS], f32r)
        h_lo = sb("h_lo", [128, KC, TOKENS], f32r)
        rw_raw = sb("rw_raw", [128, KC, LOGITS])
        rw_hi = sb("rw_hi", [128, KC, LOGITS], f32r)
        rw_lo = sb("rw_lo", [128, KC, LOGITS], f32r)
        top8 = sb("top8", [128, BLOCKS, TOP])
        shifted = sb("shifted", [128, BLOCKS, 2, EXPERTS])
        small = sb("small", [128, 2, 4 * TOP + 4])
        denom = sb("denom", [128, 2, 8])
        recip = sb("recip", [128, 2, 8])
        route = sb("route", [128, BLOCKS, EXPERTS + 1])
        route_t = sb("route_t", [EXPERTS + 1, TOKENS])
        ident = sb("ident", [128, 128])
        gu_raw = sb("gu_raw", [128, 2, KC * 256])
        gu_hi = sb("gu_hi", [128, 2, KC * 256], f32r)
        gu_lo = sb("gu_lo", [128, 2, KC * 256], f32r)
        dp_raw = sb("dp_raw", [128, 2, TIME])
        dp_hi = sb("dp_hi", [128, 2, TIME], f32r)
        dp_lo = sb("dp_lo", [128, 2, TIME], f32r)
        route_bc = sb("route_bc", [128, 2, TOKENS])
        silu_sb = sb("silu_sb", [128, 2, HALF])
        inter = sb("inter", [128, SLOTS, HALF])
        inter_hi = sb("inter_hi", [128, SLOTS, HALF], f32r)
        inter_lo = sb("inter_lo", [128, SLOTS, HALF], f32r)
        xt_sb = sb("xt_sb", [128, KC, TOKENS])
        out_sb = sb("out_sb", [128, KC, TOKENS])

        acc = ps("acc", [128, KC * 2, HALF])
        gate_ps = ps("gate_ps", [128, 2, HALF])
        up_ps = ps("up_ps", [128, 2, HALF])

        itok_in = sem("itok_in")
        x_in = sem("x_in")
        rw_in = sem("rw_in")
        xt_in = sem("xt_in")
        gu_in = [sem(f"gu_in{s}") for s in range(2)]
        dp_in = [sem(f"dp_in{s}") for s in range(2)]
        route_in = [sem(f"route_in{s}") for s in range(2)]
        route_first_in = [[sem(f"route_first_in{s}{h}") for h in range(2)] for s in range(2)]
        chan_ready = sem("chan_ready")
        clamp_done = sem("clamp_done")
        table_row_ready = sem("table_row_ready")
        gather_in = [sem(f"gather_in{g}") for g in range(GROUPS)]
        diag_zero = sem("diag_zero")
        diag_ready = sem("diag_ready")
        ident_step = sem("ident_step")
        h_ps_ready = sem("h_ps_ready")
        h_hi_ready = sem("h_hi_ready")
        h_ready = sem("h_ready")
        rw_hi_ready = sem("rw_hi_ready")
        rw_ready = sem("rw_ready")
        logits_ready = sem("logits_ready")
        router_step = sem("router_step")
        shifted_ready = sem("shifted_ready")
        exp_ready = sem("exp_ready")
        route_ready = sem("route_ready")
        route_t_ps_ready = sem("route_t_ps_ready")
        route_t_ready = sem("route_t_ready")
        route_out = sem("route_out")
        gu_hi_ready = sem("gu_hi_ready")
        gu_ready = sem("gu_ready")
        dp_hi_ready = sem("dp_hi_ready")
        dp_ready = sem("dp_ready")
        gate_done = sem("gate_done")
        up_done = sem("up_done")
        silu_done = sem("silu_done")
        gated = sem("gated")
        weighted = sem("weighted")
        inter_hi_ready = sem("inter_hi_ready")
        inter_ready = sem("inter_ready")
        down_done = sem("down_done")
        acc_done = sem("acc_done")
        out_ready = sem("out_ready")
        stored = sem("stored")

        block = ctx.enter_context(nc.Block())

        @block.sync
        def _(sp):
            for j in range(2):
                sp.dma_start(itok_sb[32 * j:32 * j + 32, :], itok[j:j + 1, :].to_broadcast([32, GROUPS])
                             ).then_inc(itok_in, 16)
            sp.dma_start(x_sb[:, :, :], x.rearrange("(g p) t -> p g t", p=128)).then_inc(x_in, 16)
            sp.dma_start(rw_raw[:, :, :], router_w.rearrange("(k p) e -> p k e", p=128)).then_inc(rw_in, 16)
            def load_gu(p, s):
                sp.dma_start(gu_raw[:, s, :], gu_w[bass.ds(p, 1), :, :].rearrange("a p n -> (a p) n")
                             ).then_inc(gu_in[s], 16)

            def load_dp(p, s):
                sp.dma_start(dp_raw[:, s, :], dp_w[bass.ds(p, 1), :, :].rearrange("a p n -> (a p) n")
                             ).then_inc(dp_in[s], 16)

            load_gu(0, 0)
            load_gu(1, 1)
            load_dp(0, 0)
            load_dp(1, 1)
            sp.wait_ge(gu_ready, 1)
            load_gu(2, 0)
            sp.wait_ge(gu_ready, 2)
            load_gu(3, 1)
            sp.wait_ge(dp_ready, 1)
            load_dp(2, 0)

            def load_route(p, s, n, arrived):
                for e in range(2):
                    sp.dma_start(route_bc[64 * e:64 * e + 64, s, n],
                                 routing_dram[bass.ds(p * 2 + e, 1), n].to_broadcast([64, n.stop - n.start])
                                 ).then_inc(arrived, 16)

            for half in range(2):
                n = slice(half * HALF, (half + 1) * HALF)
                sp.wait_ge(route_t_ready, half + 1)
                sp.dma_start(routing_dram[:, n], route_t[:, n]).then_inc(route_out, 16)
                sp.wait_ge(route_out, 16 * half + 16)
                for p in range(2):
                    load_route(p, p, n, route_first_in[p][half])
            sp.dma_start(xt_sb[:, :, :], x_t.rearrange("(k p) n -> p k n", p=128)).then_inc(xt_in, 16)

            def refill_route(i, s):
                sp.wait_ge(weighted, i * 4 + (2 * s + 2))
                load_route(i * 2 + (s + 2), s, slice(0, TOKENS), route_in[s])

            def refill_gu(i, s):
                sp.wait_ge(gu_ready, i * 2 + (s + 3))
                load_gu(i * 2 + (s + 4), s)

            def refill_dp(i, s):
                sp.wait_ge(dp_ready, i * 2 + (s + 2))
                load_dp(i * 2 + (s + 3), 1 - s)

            last = PAIRS // 2 - 2
            with sp.Fori(0, last) as i:
                for s in range(2):
                    refill_route(i, s)
                    refill_gu(i, s)
                    refill_dp(i, s)
            refill_route(last, 0)
            refill_gu(last, 0)
            refill_dp(last, 0)
            refill_route(last, 1)
            refill_dp(last, 1)
            sp.wait_ge(weighted, UNITS - 2)
            sp.dma_start(route_bc[0:64, 0, :], routing_dram[EXPERTS:EXPERTS + 1, :].to_broadcast([64, TOKENS])
                         ).then_inc(route_in[0], 16)
            for n, (half, k) in enumerate([(0, 0), (0, 1), (1, 0), (1, 1)]):
                sp.wait_ge(out_ready, n + 1)
                sp.dma_start(out_t[k * 128:k * 128 + 128, half * HALF:(half + 1) * HALF],
                             out_sb[:, k, half * HALF:(half + 1) * HALF]).then_inc(stored, 16)
            sp.wait_ge(stored, 64)

        @block.gpsimd
        def _(pool):
            for j in range(4):
                pool.iota(chan_of_row[32 * j:32 * j + 32, :], pattern=[[0, 1]], base=0, channel_multiplier=1,
                          allow_small_or_imprecise_dtypes=True).then_inc(chan_ready, 1)
            pool.wait_ge(chan_ready, 4)
            pool.memset(ident[:, :], 0.0).then_inc(ident_step, 1)
            pool.wait_ge(ident_step, 1)
            pool.affine_select(out=ident[:, :], in_=ident[:, :], compare_op=ALU.not_equal, fill=1.0,
                               base=0, pattern=[[-1, 128]], channel_multiplier=1).then_inc(ident_step, 1)
            pool.wait_ge(table_row_ready, 1)
            for g in range(GROUPS):
                pool.indirect_dma_start(
                    out=gathered[:, g, :], out_offset=None, in_=cond_w,
                    in_offset=bass.IndirectOffsetOnAxis(ap=table_row[:, g:g + 1], axis=0),
                    bounds_check=STATES * CHAN - 1, oob_is_err=False).then_inc(gather_in[g], 16)

            def weight(i, j, first):
                s, half = j // 2, j % 2
                pool.wait_ge(gated, i * 4 + (j + 1))
                if first:
                    pool.wait_ge(route_first_in[s][half], 32)
                elif half == 0:
                    pool.wait_ge(route_in[s], i * 32)
                pool.tensor_tensor(inter[:, j, :], inter[:, j, :],
                                   route_bc[:, s, half * HALF:(half + 1) * HALF], ALU.mult
                                   ).then_inc(weighted, 1)

            for j in range(SLOTS):
                weight(0, j, True)
            with pool.Fori(1, PAIRS // 2) as i:
                for j in range(SLOTS):
                    weight(i, j, False)
            pool.wait_ge(route_in[0], 16 * PAIRS - 16)
            for half in range(2):
                pool.wait_ge(gated, UNITS + half + 1)
                pool.tensor_tensor(inter[0:64, half, :], inter[0:64, half, :],
                                   route_bc[0:64, 0, half * HALF:(half + 1) * HALF], ALU.mult
                                   ).then_inc(weighted, 1)

        @block.scalar
        def _(act):
            for j in range(2, 4):
                act.dma_start(itok_sb[32 * j:32 * j + 32, :], itok[j:j + 1, :].to_broadcast([32, GROUPS])
                              ).then_inc(itok_in, 16)
            act.wait_ge(rw_in, 16)
            act.activation(rw_hi[:, :, :], rw_raw[:, :, :], ACT.Copy).then_inc(rw_hi_ready, 1)

            def split_gu(i, s, first):
                act.wait_ge(gu_in[s], i * 16 + 16)
                if not first:
                    act.wait_ge(up_done, i * 4 + (2 * s - 2))
                act.activation(gu_hi[:, s, :], gu_raw[:, s, :], ACT.Copy).then_inc(gu_hi_ready, 1)

            def split_dp(i, s, first):
                act.wait_ge(dp_in[s], i * 16 + 16)
                if not first:
                    act.wait_ge(down_done, i * 4 + (2 * s - 2))
                act.activation(dp_hi[:, s, :], dp_raw[:, s, :], ACT.Copy).then_inc(dp_hi_ready, 1)

            def silu(i, j, first):
                act.wait_ge(gate_done, i * 4 + (j + 1))
                if not (first and j < 2):
                    act.wait_ge(gated, i * 4 + (j - 1))
                act.activation(silu_sb[:, j % 2, :], gate_ps[:, j % 2, :], ACT.Silu).then_inc(silu_done, 1)

            def inter_split(i, j, first):
                act.wait_ge(weighted, i * 4 + (j + 1))
                if not first:
                    act.wait_ge(down_done, i * 4 + (j - 3))
                act.activation(inter_hi[:, j % SLOTS, :], inter[:, j % SLOTS, :], ACT.Copy
                               ).then_inc(inter_hi_ready, 1)

            def h_split(half):
                for k in range(KC):
                    act.wait_ge(h_ps_ready, half + 1)
                    act.activation(h_hi[:, k, half * HALF:(half + 1) * HALF], acc[:, 2 * k + half, :], ACT.Copy
                                   ).then_inc(h_hi_ready, 1)

            def router_exp(half):
                act.wait_ge(shifted_ready, half + 1)
                act.activation(small[:, half, :], small[:, half, :], ACT.Exp).then_inc(exp_ready, 1)
                act.activation(shifted[:, 4 * half:4 * half + 4, :, :], shifted[:, 4 * half:4 * half + 4, :, :],
                               ACT.Exp).then_inc(exp_ready, 1)

            split_gu(0, 0, True)
            split_gu(0, 1, True)
            split_dp(0, 0, True)
            split_dp(0, 1, True)
            h_split(0)
            h_split(1)
            router_exp(0)
            router_exp(1)
            for j in range(SLOTS):
                silu(0, j, True)
            split_gu(1, 0, False)
            for j in range(3):
                inter_split(0, j, True)
            with act.Fori(1, PAIRS // 2) as i:
                for j in range(SLOTS):
                    silu(i, j, False)
                    if j == 0:
                        inter_split(i - 1, 3, False)
                        split_gu(i, 1, False)
                    if j == 1:
                        inter_split(i, 0, False)
                        split_dp(i, 0, False)
                    if j == 2:
                        inter_split(i, 1, False)
                        split_gu(i + 1, 0, False)
                    if j == 3:
                        inter_split(i, 2, False)
                        split_dp(i, 1, False)
            last = PAIRS // 2
            inter_split(last - 1, 3, False)
            for half in range(2):
                act.wait_ge(gate_done, UNITS + half + 1)
                act.wait_ge(gated, UNITS + half - 1)
                act.activation(silu_sb[0:64, half, :], gate_ps[0:64, half, :], ACT.Silu).then_inc(silu_done, 1)
                if half == 0:
                    split_dp(last, 0, False)
            for half in range(2):
                act.wait_ge(weighted, UNITS + half + 1)
                act.wait_ge(down_done, UNITS + half - 3)
                act.activation(inter_hi[0:64, half, :], inter[0:64, half, :], ACT.Copy).then_inc(inter_hi_ready, 1)

        @block.vector
        def _(dve):
            dve.memset(diag[:, :, :], 0.0).then_inc(diag_zero, 1)
            dve.wait_ge(itok_in, 64)
            dve.tensor_scalar(clamped[:, :], itok_sb[:, :], 0.0, float(STATES - 1), ALU.max, ALU.min
                              ).then_inc(clamp_done, 1)
            dve.wait_ge(clamp_done, 1)
            dve.wait_ge(chan_ready, 4)
            dve.tensor_scalar(table_row[:, :], clamped[:, :], float(CHAN), chan_of_row[:, 0:1], ALU.mult, ALU.add
                              ).then_inc(table_row_ready, 1)
            dve.wait_ge(rw_hi_ready, 1)
            dve.tensor_tensor(rw_lo[:, :, :], rw_raw[:, :, :], rw_hi[:, :, :].bitcast(f32), ALU.subtract
                              ).then_inc(rw_ready, 1)
            dve.wait_ge(diag_zero, 1)

            def fill_diag(g):
                dve.wait_ge(gather_in[g], 16)
                for j in range(4):
                    r = slice(32 * j, 32 * j + 32)
                    dve.tensor_copy(diag[r, g, 32 * j:32 * j + 32], gathered[r, g, :]).then_inc(diag_ready, 1)

            def h_split(half):
                hs = slice(half * HALF, (half + 1) * HALF)
                for k in range(KC):
                    dve.wait_ge(h_hi_ready, 2 * half + k + 1)
                    dve.tensor_tensor(h_lo[:, k, hs], acc[:, 2 * k + half, :], h_hi[:, k, hs].bitcast(f32),
                                      ALU.subtract).then_inc(h_ready, 1)

            def split_gu(i, s):
                dve.wait_ge(gu_hi_ready, i * 2 + (s + 1))
                dve.tensor_tensor(gu_lo[:, s, :], gu_raw[:, s, :], gu_hi[:, s, :].bitcast(f32), ALU.subtract
                                  ).then_inc(gu_ready, 1)

            def split_dp(i, s):
                dve.wait_ge(dp_hi_ready, i * 2 + (s + 1))
                dve.tensor_tensor(dp_lo[:, s, :], dp_raw[:, s, :], dp_hi[:, s, :].bitcast(f32), ALU.subtract
                                  ).then_inc(dp_ready, 1)

            def gate(i, j, first):
                dve.wait_ge(silu_done, i * 4 + (j + 1))
                dve.wait_ge(up_done, i * 4 + (j + 1))
                if not first:
                    dve.wait_ge(inter_ready, i * 4 + (j - 3))
                dve.tensor_tensor(inter[:, j, :], silu_sb[:, j % 2, :], up_ps[:, j % 2, :], ALU.mult
                                  ).then_inc(gated, 1)

            def inter_split(i, j):
                dve.wait_ge(inter_hi_ready, i * 4 + (j + 1))
                dve.tensor_tensor(inter_lo[:, j, :], inter[:, j, :], inter_hi[:, j, :].bitcast(f32), ALU.subtract
                                  ).then_inc(inter_ready, 1)

            steps = [0]

            def step(ins):
                steps[0] += 1
                ins.then_inc(router_step, 1)

            def router_shift(half):
                b4 = slice(4 * half, 4 * half + 4)
                logits = acc[:, half, 0:4 * LOGITS].rearrange("p (b e) -> p b e", b=4)
                dve.wait_ge(logits_ready, half + 1)
                for b in range(4):
                    step(dve.max(top8[:, 4 * half + b, :], logits[:, b, 0:EXPERTS]))
                step(dve.tensor_scalar(small[:, half, 4 * TOP:4 * TOP + 4], logits[:, :, EXPERTS], -1.0, None,
                                       ALU.mult))
                dve.wait_ge(router_step, steps[0] - 1)
                for b in range(4):
                    step(dve.match_replace(shifted[:, 4 * half + b, 1, :], top8[:, 4 * half + b, :],
                                           logits[:, b, 0:EXPERTS], -3.0e38))
                step(dve.tensor_tensor(small[:, half, 0:4 * TOP].rearrange("p (b e) -> p b e", b=4),
                                       top8[:, b4, :], top8[:, b4, 0:1].to_broadcast([128, 4, TOP]), ALU.subtract))
                step(dve.tensor_tensor(shifted[:, b4, 0, :], logits[:, :, 0:EXPERTS],
                                       top8[:, b4, 0:1].to_broadcast([128, 4, EXPERTS]), ALU.subtract))
                dve.wait_ge(router_step, steps[0])
                dve.tensor_tensor(shifted[:, b4, 1, :], shifted[:, b4, 1, :],
                                  top8[:, b4, 0:1].to_broadcast([128, 4, EXPERTS]), ALU.subtract
                                  ).then_inc(shifted_ready, 1)

            def router_normalise(half):
                b4 = slice(4 * half, 4 * half + 4)
                dve.wait_ge(exp_ready, 2 * half + 1)
                step(dve.tensor_reduce(denom[:, half, 0:4],
                                       small[:, half, 0:4 * TOP].rearrange("p (b e) -> p b e", b=4), AX.X, ALU.add))
                step(dve.tensor_scalar(denom[:, half, 4:8], small[:, half, 4 * TOP:4 * TOP + 4], 1.0, None, ALU.add))
                dve.wait_ge(router_step, steps[0])
                step(dve.reciprocal(recip[:, half, :], denom[:, half, :]))
                dve.wait_ge(exp_ready, 2 * half + 2)
                step(dve.tensor_tensor(route[:, b4, 0:EXPERTS], shifted[:, b4, 0, :], shifted[:, b4, 1, :],
                                       ALU.subtract))
                dve.wait_ge(router_step, steps[0])
                dve.tensor_copy(route[:, b4, EXPERTS], recip[:, half, 4:8]).then_inc(route_ready, 1)
                dve.tensor_tensor(route[:, b4, 0:EXPERTS], route[:, b4, 0:EXPERTS],
                                  recip[:, half, 0:4].rearrange("p (b e) -> p b e", e=1)
                                  .to_broadcast([128, 4, EXPERTS]), ALU.mult).then_inc(route_ready, 1)

            def route_t_copy(half):
                dve.wait_ge(route_t_ps_ready, half + 1)
                dve.tensor_copy(route_t[:, half * HALF:(half + 1) * HALF], acc[0:EXPERTS + 1, 2 + half, :]
                                ).then_inc(route_t_ready, 1)

            split_gu(0, 0)
            for g in range(GROUPS // 2):
                fill_diag(g)
            split_gu(0, 1)
            for g in range(GROUPS // 2, GROUPS):
                fill_diag(g)
            h_split(0)
            h_split(1)
            split_dp(0, 0)
            split_dp(0, 1)
            router_shift(0)
            router_normalise(0)
            router_shift(1)
            route_t_copy(0)
            router_normalise(1)
            gate(0, 0, True)
            route_t_copy(1)
            gate(0, 1, True)
            gate(0, 2, True)
            gate(0, 3, True)
            split_gu(1, 0)
            for j in range(3):
                inter_split(0, j)
            with dve.Fori(1, PAIRS // 2) as i:
                for j in range(SLOTS):
                    gate(i, j, False)
                    if j == 0:
                        inter_split(i - 1, 3)
                        split_gu(i, 1)
                    if j == 1:
                        inter_split(i, 0)
                        split_dp(i, 0)
                    if j == 2:
                        inter_split(i, 1)
                        split_gu(i + 1, 0)
                    if j == 3:
                        inter_split(i, 2)
                        split_dp(i, 1)
            last = PAIRS // 2
            inter_split(last - 1, 3)
            for half in range(2):
                dve.wait_ge(silu_done, UNITS + half + 1)
                dve.wait_ge(inter_ready, UNITS + half - 3)
                dve.tensor_tensor(inter[0:64, half, :], silu_sb[0:64, half, :], gate_ps[64:128, half, :], ALU.mult
                                  ).then_inc(gated, 1)
                if half == 0:
                    split_dp(last, 0)
            for half in range(2):
                dve.wait_ge(inter_hi_ready, UNITS + half + 1)
                dve.tensor_tensor(inter_lo[0:64, half, :], inter[0:64, half, :],
                                  inter_hi[0:64, half, :].bitcast(f32), ALU.subtract).then_inc(inter_ready, 1)
            dve.wait_ge(xt_in, 16)
            for n, (half, k) in enumerate([(0, 0), (0, 1), (1, 0), (1, 1)]):
                hs = slice(half * HALF, (half + 1) * HALF)
                dve.wait_ge(acc_done, n + 1)
                dve.tensor_tensor(out_sb[:, k, hs], acc[:, 2 * k + half, :], xt_sb[:, k, hs], ALU.add
                                  ).then_inc(out_ready, 1)

        @block.tensor
        def _(pe):
            def passes(out, w_hi, w_lo, m_hi, m_lo, start, stop):
                pe.matmul(out, w_hi, m_hi, start=start, stop=False)
                pe.matmul(out, w_hi, m_lo, start=False, stop=False)
                return pe.matmul(out, w_lo, m_hi, start=False, stop=stop)

            def condition(half):
                for g in range(GROUPS // 2):
                    gg = half * (GROUPS // 2) + g
                    pe.wait_ge(diag_ready, 4 * gg + 4)
                    for k in range(KC):
                        mm = pe.matmul(acc[:, 2 * k + half, g * 128:g * 128 + 128],
                                       x_sb[:, gg, k * 128:k * 128 + 128], diag[:, gg, :], start=True, stop=True)
                mm.then_inc(h_ps_ready, 1)

            def logits(half):
                pe.wait_ge(h_ready, 2 * half + 2)
                for b in range(4):
                    n = slice((4 * half + b) * 128, (4 * half + b + 1) * 128)
                    for k in range(KC):
                        mm = passes(acc[:, half, b * LOGITS:(b + 1) * LOGITS], h_hi[:, k, n], h_lo[:, k, n],
                                    rw_hi[:, k, :], rw_lo[:, k, :], k == 0, k == KC - 1)
                mm.then_inc(logits_ready, 1)

            def route_transpose(half):
                pe.wait_ge(route_ready, 2 * half + 2)
                for b in range(4):
                    mm = pe.transpose(acc[0:EXPERTS + 1, 2 + half, b * 128:b * 128 + 128],
                                      route[:, 4 * half + b, :], ident[:, :])
                mm.then_inc(route_t_ps_ready, 1)

            def product(i, j, part, bank, done):
                s, half = j // 2, j % 2
                for k in range(KC):
                    w = slice(k * 256 + part * 128, k * 256 + part * 128 + 128)
                    n = slice(half * HALF, (half + 1) * HALF)
                    mm = passes(bank[:, half, :], gu_hi[:, s, w], gu_lo[:, s, w], h_hi[:, k, n], h_lo[:, k, n],
                                k == 0, k == KC - 1)
                mm.then_inc(done, 1)

            def gate_up(i, j, first):
                if j % 2 == 0:
                    pe.wait_ge(gu_ready, i * 2 + (j // 2 + 1))
                if not (first and j < 2):
                    pe.wait_ge(gated, i * 4 + (j - 1))
                product(i, j, 0, gate_ps, gate_done)
                product(i, j, 1, up_ps, up_done)

            def down(i, j, first):
                s, half = j // 2, j % 2
                if half == 0:
                    pe.wait_ge(dp_ready, i * 2 + (s + 1))
                pe.wait_ge(inter_ready, i * 4 + (j + 1))
                for k in range(KC):
                    w = slice(k * 128, k * 128 + 128)
                    mm = passes(acc[:, 2 * k + half, :], dp_hi[:, s, w], dp_lo[:, s, w],
                                inter_hi[:, j, :], inter_lo[:, j, :], first and s == 0, False)
                mm.then_inc(down_done, 1)

            pe.wait_ge(ident_step, 2)
            with pe.Fori(0, WARM_UP) as _:
                pe.matmul(gate_ps[:, 0, 0:128], ident[:, :], ident[:, :], start=True, stop=True)
            pe.wait_ge(x_in, 16)
            condition(0)
            condition(1)
            pe.wait_ge(rw_ready, 1)
            logits(0)
            logits(1)
            gate_up(0, 0, True)
            route_transpose(0)
            gate_up(0, 1, True)
            route_transpose(1)
            gate_up(0, 2, True)
            gate_up(0, 3, True)
            for j in range(SLOTS):
                gate_up(1, j, False)
                down(0, j, True)
            with pe.Fori(2, PAIRS // 2) as i:
                for j in range(SLOTS):
                    gate_up(i, j, False)
                    down(i - 1, j, False)
            last = PAIRS // 2
            pe.wait_ge(gu_ready, PAIRS + 1)
            for half in range(2):
                pe.wait_ge(gated, UNITS + half - 1)
                for k in range(KC):
                    w = slice(k * 256, k * 256 + 128)
                    n = slice(half * HALF, (half + 1) * HALF)
                    mm = passes(gate_ps[:, half, :], gu_hi[:, 0, w], gu_lo[:, 0, w], h_hi[:, k, n], h_lo[:, k, n],
                                k == 0, k == KC - 1)
                mm.then_inc(gate_done, 1)
                down(last - 1, half, False)
            for j in range(2, SLOTS):
                down(last - 1, j, False)
            pe.wait_ge(dp_ready, PAIRS + 1)
            for half in range(2):
                pe.wait_ge(inter_ready, UNITS + half + 1)
                for k in range(KC):
                    w = slice(k * 128, k * 128 + 128)
                    passes(acc[:, 2 * k + half, :], dp_hi[0:64, 0, w], dp_lo[0:64, 0, w],
                           inter_hi[0:64, half, :], inter_lo[0:64, half, :], False, True).then_inc(acc_done, 1)


def kernel(x, itok_B_1_198, L0_cond_weights, L0_ffn_gate_w, L0_ffn_gu_w, L0_ffn_dp_w, L0_ffn_sh_gate_w,
           L0_ffn_sh_up_w, L0_ffn_sh_down_w, L0_ffn_sh_gate1_w):
    import numpy as np
    import concourse.bacc as bacc
    from concourse.bass_utils import run_bass_kernel_spmd

    x, gu, dp = np.asarray(x), np.asarray(L0_ffn_gu_w), np.asarray(L0_ffn_dp_w)
    sh_gate, sh_up, sh_down = map(np.asarray, (L0_ffn_sh_gate_w, L0_ffn_sh_up_w, L0_ffn_sh_down_w))
    f32 = gu.dtype

    gu_all = np.zeros((PAIRS + 1, 128, KC, 2, 128), f32)
    gu_all[:PAIRS] = gu.reshape(PAIRS, 2, 2, INNER, KC, 128).transpose(0, 5, 4, 2, 1, 3).reshape(
        PAIRS, 128, KC, 2, 128)
    gu_all[PAIRS, :, :, 0, :INNER] = sh_gate.reshape(INNER, KC, 128).transpose(2, 1, 0)
    gu_all[PAIRS, :, :, 0, INNER:] = sh_up.reshape(INNER, KC, 128).transpose(2, 1, 0)
    dp_all = np.zeros((PAIRS + 1, 128, TIME), f32)
    dp_all[:PAIRS] = dp.reshape(PAIRS, 2, TIME, INNER).transpose(0, 1, 3, 2).reshape(PAIRS, 128, TIME)
    dp_all[PAIRS, :INNER] = sh_down.T
    router = np.zeros((TIME, LOGITS), f32)
    router[:, :EXPERTS] = np.asarray(L0_ffn_gate_w).T
    router[:, EXPERTS] = np.asarray(L0_ffn_sh_gate1_w)[0]

    arrays = {
        "x": np.ascontiguousarray(x.reshape(BATCH * CHAN, TIME)),
        "x_t": np.ascontiguousarray(x.reshape(TOKENS, TIME).T),
        "itok": np.ascontiguousarray(np.asarray(itok_B_1_198).reshape(GROUPS, 4).T),
        "cond_w": np.ascontiguousarray(np.asarray(L0_cond_weights).reshape(STATES * CHAN, COND)),
        "router_w": router,
        "gu_w": gu_all.reshape(PAIRS + 1, 128, KC * 256),
        "dp_w": dp_all,
    }
    nc = bacc.Bacc("TRN2", target_bir_lowering=False, num_devices=1)
    args = [nc.dram_tensor(f"in_{n}", a.shape, mybir.dt.from_np(a.dtype), kind="ExternalInput").ap()
            for n, a in arrays.items()]
    out = nc.dram_tensor("out_t", (TIME, TOKENS), mybir.dt.from_np(x.dtype), kind="ExternalOutput").ap()
    adaln_moe_kernel(nc, *args, out)
    r = run_bass_kernel_spmd(nc, [{f"in_{n}": a for n, a in arrays.items()}], core_ids=[0])
    return np.ascontiguousarray(r.results[0]["out_t"].T).reshape(x.shape)
```

```python
from contextlib import ExitStack

import concourse.bass as bass
from concourse import mybir

BATCH, CHAN, TIME = 32, 32, 256
STATES, COND = 200, 32
TOKENS = BATCH * COND
HALF = TOKENS // 2
KC = TIME // 128
EXPERTS, INNER, TOP = 64, 64, 8
PAIRS = EXPERTS // 2
LOGITS = EXPERTS + 2
BLOCKS = TOKENS // 128
GROUPS = BATCH * CHAN // 128
SLOTS = 4
WARM_UP = 16
UNITS = 2 * PAIRS
LAG = 3


def adaln_moe_kernel(nc, x, x_t, itok, cond_w, router_w, gu_w, dp_w, sh_gu_w, sh_dp_w, out_t):
    f32, f32r, i32 = mybir.dt.float32, mybir.dt.float32r, mybir.dt.int32
    ALU = mybir.AluOpType
    ACT = mybir.ActivationFunctionType
    AX = mybir.AxisListType

    routing_dram = nc.dram_tensor("routing_dram", (EXPERTS + 1, TOKENS), f32, kind="Internal").ap()

    PIECES = [(0, 0, slice(0, HALF)), (0, 1, slice(0, HALF)), (1, 0, slice(HALF, TOKENS)),
              (1, 1, slice(HALF, HALF + HALF // 2)), (1, 1, slice(HALF + HALF // 2, TOKENS))]

    ctx = ExitStack()
    with ctx:
        def sb(name, shape, dt=f32):
            return ctx.enter_context(nc.sbuf_tensor(name, shape, dt))

        def ps(name, shape, dt=f32):
            return ctx.enter_context(nc.psum_tensor(name, shape, dt))

        def sem(name):
            return ctx.enter_context(nc.semaphore(name))

        x_sb = sb("x_sb", [128, GROUPS, TIME])
        itok_sb = sb("itok_sb", [BATCH, 1], i32)
        table_row = sb("table_row", [BATCH, 1], i32)
        gathered = sb("gathered", [BATCH, CHAN * COND])
        turned = sb("turned", [CHAN, COND, BATCH])
        diag = sb("diag", [128, GROUPS, 128])
        h_hi = sb("h_hi", [128, KC, TOKENS], f32r)
        h_lo = sb("h_lo", [128, KC, TOKENS], f32r)
        rw_raw = sb("rw_raw", [128, KC, LOGITS])
        rw_hi = sb("rw_hi", [128, KC, LOGITS], f32r)
        rw_lo = sb("rw_lo", [128, KC, LOGITS], f32r)
        top8 = sb("top8", [128, BLOCKS, TOP])
        shifted = sb("shifted", [128, BLOCKS, 2, EXPERTS])
        small = sb("small", [128, 2, 4 * TOP + 4])
        denom = sb("denom", [128, 2, 8])
        recip = sb("recip", [128, 2, 8])
        route = sb("route", [128, BLOCKS, EXPERTS + 1])
        logit_t = sb("logit_t", [LOGITS, TOKENS])
        route_t = sb("route_t", [EXPERTS + 1, TOKENS])
        ident = sb("ident", [128, 128])
        gu_raw = sb("gu_raw", [128, 2, KC * 256])
        gu_hi = sb("gu_hi", [128, 2, KC * 256], f32r)
        gu_lo = sb("gu_lo", [128, 2, KC * 256], f32r)
        dp_raw = sb("dp_raw", [128, 2, TIME])
        dp_hi = sb("dp_hi", [128, 2, TIME], f32r)
        dp_lo = sb("dp_lo", [128, 2, TIME], f32r)
        route_bc = sb("route_bc", [128, 2, TOKENS])
        silu_sb = sb("silu_sb", [128, 2, HALF])
        inter = sb("inter", [128, SLOTS, HALF])
        inter_hi = sb("inter_hi", [128, SLOTS, HALF], f32r)
        inter_lo = sb("inter_lo", [128, SLOTS, HALF], f32r)
        sh_gu_raw = sb("sh_gu_raw", [128, KC * 128])
        sh_gu_hi = sb("sh_gu_hi", [128, KC * 128], f32r)
        sh_gu_lo = sb("sh_gu_lo", [128, KC * 128], f32r)
        sh_dp_raw = sb("sh_dp_raw", [128, TIME])
        sh_dp_hi = sb("sh_dp_hi", [128, TIME], f32r)
        sh_dp_lo = sb("sh_dp_lo", [128, TIME], f32r)
        sh_route_bc = sb("sh_route_bc", [INNER, TOKENS])
        sh_silu = sb("sh_silu", [INNER, 2, HALF])
        sh_inter = sb("sh_inter", [INNER, 2, HALF])
        sh_inter_parts = sb("sh_inter_parts", [128, 2, HALF], f32r)
        xt_sb = sb("xt_sb", [128, KC, TOKENS])
        out_sb = sb("out_sb", [128, KC, TOKENS])

        acc = ps("acc", [128, KC * 2, HALF])
        gate_ps = ps("gate_ps", [128, 2, HALF])
        up_ps = ps("up_ps", [128, 2, HALF])

        itok_in = sem("itok_in")
        x_in = [sem(f"x_in{h}") for h in range(2)]
        rw_in = sem("rw_in")
        xt_in = sem("xt_in")
        gu_in = [sem(f"gu_in{s}") for s in range(2)]
        dp_in = [sem(f"dp_in{s}") for s in range(2)]
        route_in = [sem(f"route_in{s}") for s in range(2)]
        route_first_in = [[sem(f"route_first_in{s}{h}") for h in range(2)] for s in range(2)]
        table_row_ready = sem("table_row_ready")
        gather_in = sem("gather_in")
        turned_ready = sem("turned_ready")
        diag_zero = sem("diag_zero")
        diag_ready = sem("diag_ready")
        ident_step = sem("ident_step")
        h_ps_ready = sem("h_ps_ready")
        h_hi_ready = sem("h_hi_ready")
        h_ready = sem("h_ready")
        rw_hi_ready = sem("rw_hi_ready")
        rw_ready = sem("rw_ready")
        logit_t_ps_ready = sem("logit_t_ps_ready")
        logit_t_ready = sem("logit_t_ready")
        logits_ready = sem("logits_ready")
        router_step = sem("router_step")
        shifted_ready = sem("shifted_ready")
        exp_ready = sem("exp_ready")
        route_ready = sem("route_ready")
        route_t_ps_ready = sem("route_t_ps_ready")
        route_t_ready = sem("route_t_ready")
        route_out = sem("route_out")
        gu_hi_ready = sem("gu_hi_ready")
        gu_ready = sem("gu_ready")
        dp_hi_ready = sem("dp_hi_ready")
        dp_ready = sem("dp_ready")
        gate_done = sem("gate_done")
        up_done = sem("up_done")
        silu_done = sem("silu_done")
        gated = sem("gated")
        weighted = sem("weighted")
        inter_hi_ready = sem("inter_hi_ready")
        inter_ready = sem("inter_ready")
        down_done = sem("down_done")
        sh_gu_in = sem("sh_gu_in")
        sh_dp_in = sem("sh_dp_in")
        sh_route_in = sem("sh_route_in")
        sh_gu_hi_ready = sem("sh_gu_hi_ready")
        sh_gu_ready = sem("sh_gu_ready")
        sh_dp_hi_ready = sem("sh_dp_hi_ready")
        sh_dp_ready = sem("sh_dp_ready")
        sh_gate_up_done = sem("sh_gate_up_done")
        sh_silu_done = sem("sh_silu_done")
        sh_gated = sem("sh_gated")
        sh_weighted = sem("sh_weighted")
        sh_inter_hi_ready = sem("sh_inter_hi_ready")
        sh_inter_ready = sem("sh_inter_ready")
        acc_done = sem("acc_done")
        out_ready = sem("out_ready")
        stored = sem("stored")

        block = ctx.enter_context(nc.Block())

        @block.sync
        def _(sp):
            sp.dma_start(itok_sb[:, :], itok).then_inc(itok_in, 16)
            sp.dma_start(rw_raw[:, :, :], router_w.rearrange("(k p) e -> p k e", p=128)).then_inc(rw_in, 16)

            def load_x(half):
                g = GROUPS // 2
                sp.dma_start(x_sb[:, half * g:half * g + g, :],
                             x[half * HALF:half * HALF + HALF, :].rearrange("(g p) t -> p g t", p=128)
                             ).then_inc(x_in[half], 16)

            def load_gu(p, s):
                sp.dma_start(gu_raw[:, s, :], gu_w[bass.ds(p, 1), :, :].rearrange("a p n -> (a p) n")
                             ).then_inc(gu_in[s], 16)

            def load_dp(p, s):
                sp.dma_start(dp_raw[:, s, :], dp_w[bass.ds(p, 1), :, :].rearrange("a p n -> (a p) n")
                             ).then_inc(dp_in[s], 16)

            load_x(0)
            sp.wait_ge(gather_in, 16)
            load_x(1)
            load_gu(0, 0)
            load_gu(1, 1)
            sp.dma_start(sh_gu_raw[:, :], sh_gu_w).then_inc(sh_gu_in, 16)
            load_dp(0, 0)
            load_dp(1, 1)
            sp.dma_start(sh_dp_raw[:, :], sh_dp_w).then_inc(sh_dp_in, 16)
            sp.wait_ge(gu_ready, 1)
            load_gu(2, 0)
            sp.wait_ge(gu_ready, 2)
            load_gu(3, 1)
            sp.wait_ge(dp_ready, 1)
            load_dp(2, 0)

            def store_route(half):
                n = slice(half * HALF, (half + 1) * HALF)
                sp.wait_ge(route_t_ready, half + 1)
                sp.dma_start(routing_dram[:, n], route_t[:, n]).then_inc(route_out, 16)

            def load_route(p, s, n, arrived):
                rows = routing_dram[bass.ds(p * 2, 2), n].rearrange("e (o n) -> e o n", o=1)
                sp.dma_start(route_bc[:, s, n], rows.to_broadcast([2, INNER, n.stop - n.start])
                             ).then_inc(arrived, 16)

            halves = [slice(0, HALF), slice(HALF, TOKENS)]
            store_route(0)
            sp.wait_ge(route_out, 16)
            load_route(0, 0, halves[0], route_first_in[0][0])
            store_route(1)
            load_route(1, 1, halves[0], route_first_in[1][0])
            sp.wait_ge(route_out, 32)
            load_route(0, 0, halves[1], route_first_in[0][1])
            load_route(1, 1, halves[1], route_first_in[1][1])
            sp.dma_start(sh_route_bc[:, :], routing_dram[EXPERTS:EXPERTS + 1, :].to_broadcast([INNER, TOKENS])
                         ).then_inc(sh_route_in, 16)

            def refill_route(i, s):
                sp.wait_ge(weighted, i * 4 + (2 * s + 2))
                load_route(i * 2 + (s + 2), s, slice(0, TOKENS), route_in[s])

            def refill_gu(i, s):
                sp.wait_ge(gu_ready, i * 2 + (s + 3))
                load_gu(i * 2 + (s + 4), s)

            def refill_dp(i, s):
                sp.wait_ge(dp_ready, i * 2 + (s + 2))
                load_dp(i * 2 + (s + 3), 1 - s)

            refill_route(0, 0)
            refill_gu(0, 0)
            refill_dp(0, 0)
            sp.dma_start(xt_sb[:, :, :], x_t.rearrange("(k p) n -> p k n", p=128)).then_inc(xt_in, 16)
            refill_route(0, 1)
            refill_gu(0, 1)
            refill_dp(0, 1)
            last = PAIRS // 2 - 2
            with sp.Fori(1, last) as i:
                for s in range(2):
                    refill_route(i, s)
                    refill_gu(i, s)
                    refill_dp(i, s)
            refill_route(last, 0)
            refill_dp(last, 0)
            refill_route(last, 1)
            for n, (half, k, cols) in enumerate(PIECES):
                sp.wait_ge(out_ready, n + 1)
                sp.dma_start(out_t[k * 128:k * 128 + 128, cols], out_sb[:, k, cols]).then_inc(stored, 16)
            sp.wait_ge(stored, 16 * len(PIECES))

        @block.gpsimd
        def _(pool):
            pool.memset(ident[:, :], 0.0).then_inc(ident_step, 1)
            pool.wait_ge(ident_step, 1)
            pool.affine_select(out=ident[:, :], in_=ident[:, :], compare_op=ALU.not_equal, fill=1.0,
                               base=0, pattern=[[-1, 128]], channel_multiplier=1).then_inc(ident_step, 1)
            pool.wait_ge(table_row_ready, 1)
            pool.indirect_dma_start(
                out=gathered[:, :], out_offset=None, in_=cond_w,
                in_offset=bass.IndirectOffsetOnAxis(ap=table_row[:, 0:1], axis=0),
                bounds_check=STATES - 1, oob_is_err=False).then_inc(gather_in, 16)

            def weight(i, j, first):
                s, half = j // 2, j % 2
                pool.wait_ge(gated, i * 4 + (j + 1))
                if first:
                    pool.wait_ge(route_first_in[s][half], 16)
                elif half == 0:
                    pool.wait_ge(route_in[s], i * 16)
                pool.tensor_tensor(inter[:, j, :], inter[:, j, :],
                                   route_bc[:, s, half * HALF:(half + 1) * HALF], ALU.mult
                                   ).then_inc(weighted, 1)

            for j in range(SLOTS):
                weight(0, j, True)
            pool.wait_ge(sh_route_in, 16)
            for half in range(2):
                pool.wait_ge(sh_gated, half + 1)
                pool.tensor_tensor(sh_inter[:, half, :], sh_inter[:, half, :],
                                   sh_route_bc[:, half * HALF:(half + 1) * HALF], ALU.mult
                                   ).then_inc(sh_weighted, 1)
            with pool.Fori(1, PAIRS // 2) as i:
                for j in range(SLOTS):
                    weight(i, j, False)

        @block.scalar
        def _(act):
            act.wait_ge(rw_in, 16)
            act.activation(rw_hi[:, :, :], rw_raw[:, :, :], ACT.Copy).then_inc(rw_hi_ready, 1)

            def split_gu(i, s, first):
                act.wait_ge(gu_in[s], i * 16 + 16)
                if not first:
                    act.wait_ge(up_done, i * 4 + (2 * s - 2))
                act.activation(gu_hi[:, s, :], gu_raw[:, s, :], ACT.Copy).then_inc(gu_hi_ready, 1)

            def split_dp(i, s, first):
                act.wait_ge(dp_in[s], i * 16 + 16)
                if not first:
                    act.wait_ge(down_done, i * 4 + (2 * s - 2))
                act.activation(dp_hi[:, s, :], dp_raw[:, s, :], ACT.Copy).then_inc(dp_hi_ready, 1)

            def silu(i, j, first):
                act.wait_ge(gate_done, i * 4 + (j + 1))
                if not (first and j < 2):
                    act.wait_ge(gated, i * 4 + (j - 1))
                act.activation(silu_sb[:, j % 2, :], gate_ps[:, j % 2, :], ACT.Silu).then_inc(silu_done, 1)

            def inter_split(i, j, first):
                act.wait_ge(weighted, i * 4 + (j + 1))
                if not first:
                    act.wait_ge(down_done, i * 4 + (j - 3))
                act.activation(inter_hi[:, j % SLOTS, :], inter[:, j % SLOTS, :], ACT.Copy
                               ).then_inc(inter_hi_ready, 1)

            def h_split(half):
                for k in range(KC):
                    act.wait_ge(h_ps_ready, 2 * half + k + 1)
                    act.activation(h_hi[:, k, half * HALF:(half + 1) * HALF], acc[:, 2 * k + half, :], ACT.Copy
                                   ).then_inc(h_hi_ready, 1)

            def logit_t_copy(half):
                act.wait_ge(logit_t_ps_ready, half + 1)
                act.activation(logit_t[:, half * HALF:(half + 1) * HALF], acc[0:LOGITS, half, :], ACT.Copy
                               ).then_inc(logit_t_ready, 1)

            def route_t_copy(half):
                act.wait_ge(route_t_ps_ready, half + 1)
                act.activation(route_t[:, half * HALF:(half + 1) * HALF], acc[0:EXPERTS + 1, half, :], ACT.Copy
                               ).then_inc(route_t_ready, 1)

            def router_exp(half):
                act.wait_ge(shifted_ready, half + 1)
                act.activation(small[:, half, :], small[:, half, :], ACT.Exp).then_inc(exp_ready, 1)
                act.activation(shifted[:, 4 * half:4 * half + 4, :, :], shifted[:, 4 * half:4 * half + 4, :, :],
                               ACT.Exp).then_inc(exp_ready, 1)

            def shared_split_gu():
                act.wait_ge(sh_gu_in, 16)
                act.activation(sh_gu_hi[:, :], sh_gu_raw[:, :], ACT.Copy).then_inc(sh_gu_hi_ready, 1)

            def shared_split_dp():
                act.wait_ge(sh_dp_in, 16)
                act.activation(sh_dp_hi[:, :], sh_dp_raw[:, :], ACT.Copy).then_inc(sh_dp_hi_ready, 1)

            def shared_silu(half):
                act.wait_ge(sh_gate_up_done, half + 1)
                act.activation(sh_silu[:, half, :], gate_ps[0:INNER, half, :], ACT.Silu).then_inc(sh_silu_done, 1)

            def shared_inter_split(half):
                act.wait_ge(sh_weighted, half + 1)
                act.activation(sh_inter_parts[0:INNER, half, :], sh_inter[:, half, :], ACT.Copy
                               ).then_inc(sh_inter_hi_ready, 1)

            h_split(0)
            split_gu(0, 0, True)
            h_split(1)
            split_gu(0, 1, True)
            logit_t_copy(0)
            shared_split_gu()
            logit_t_copy(1)
            split_dp(0, 0, True)
            split_dp(0, 1, True)
            router_exp(0)
            silu(0, 0, True)
            silu(0, 1, True)
            route_t_copy(0)
            split_gu(1, 0, False)
            silu(0, 2, True)
            router_exp(1)
            silu(0, 3, True)
            route_t_copy(1)
            shared_silu(0)
            shared_silu(1)
            shared_split_dp()

            def slot(i, j, first=False, end=False):
                silu(i, j, False)
                if j == 0:
                    split_gu(i, 1, False)
                if j == 2 and not end:
                    split_gu(i + 1, 0, False)
                if j >= LAG:
                    inter_split(i, j - LAG, False)
                else:
                    inter_split(i - 1, j - LAG + SLOTS, first)
                if j % 2 == 1:
                    split_dp(i, j // 2, False)

            inter_split(0, 0, True)
            for j in range(SLOTS):
                slot(1, j, first=True)
            for half in range(2):
                shared_inter_split(half)
            with act.Fori(2, PAIRS // 2 - 1) as i:
                for j in range(SLOTS):
                    slot(i, j)
            for j in range(SLOTS):
                slot(PAIRS // 2 - 1, j, end=True)
            for j in range(SLOTS - LAG, SLOTS):
                inter_split(PAIRS // 2 - 1, j, False)

        @block.vector
        def _(dve):
            dve.memset(diag[:, :, :], 0.0).then_inc(diag_zero, 1)
            dve.wait_ge(itok_in, 16)
            dve.tensor_scalar(table_row[:, :], itok_sb[:, :], 0.0, float(STATES - 1), ALU.max, ALU.min
                              ).then_inc(table_row_ready, 1)
            dve.wait_ge(gather_in, 16)
            dve.transpose(turned[:, :, :], gathered[:, :].rearrange("b (c d) -> b d c", d=COND)
                          ).then_inc(turned_ready, 1)
            dve.wait_ge(diag_zero, 1)
            dve.wait_ge(turned_ready, 1)
            by_place = turned[:, :, :].rearrange("c d (g j) -> c j g d", j=4)
            for half in range(2):
                g = slice(4 * half, 4 * half + 4)
                for j in range(4):
                    dve.tensor_copy(diag[32 * j:32 * j + 32, g, 32 * j:32 * j + 32], by_place[:, j, g, :]
                                    ).then_inc(diag_ready, 1)
            dve.wait_ge(rw_hi_ready, 1)
            dve.tensor_tensor(rw_lo[:, :, :], rw_raw[:, :, :], rw_hi[:, :, :].bitcast(f32), ALU.subtract
                              ).then_inc(rw_ready, 1)

            def h_split(half):
                hs = slice(half * HALF, (half + 1) * HALF)
                for k in range(KC):
                    dve.wait_ge(h_hi_ready, 2 * half + k + 1)
                    dve.tensor_tensor(h_lo[:, k, hs], acc[:, 2 * k + half, :], h_hi[:, k, hs].bitcast(f32),
                                      ALU.subtract).then_inc(h_ready, 1)

            def split_gu(i, s):
                dve.wait_ge(gu_hi_ready, i * 2 + (s + 1))
                dve.tensor_tensor(gu_lo[:, s, :], gu_raw[:, s, :], gu_hi[:, s, :].bitcast(f32), ALU.subtract
                                  ).then_inc(gu_ready, 1)

            def split_dp(i, s):
                dve.wait_ge(dp_hi_ready, i * 2 + (s + 1))
                dve.tensor_tensor(dp_lo[:, s, :], dp_raw[:, s, :], dp_hi[:, s, :].bitcast(f32), ALU.subtract
                                  ).then_inc(dp_ready, 1)

            def gate(i, j, first):
                dve.wait_ge(silu_done, i * 4 + (j + 1))
                dve.wait_ge(up_done, i * 4 + (j + 1))
                if not first:
                    dve.wait_ge(inter_ready, i * 4 + (j - 3))
                dve.tensor_tensor(inter[:, j, :], silu_sb[:, j % 2, :], up_ps[:, j % 2, :], ALU.mult
                                  ).then_inc(gated, 1)

            def inter_split(i, j):
                dve.wait_ge(inter_hi_ready, i * 4 + (j + 1))
                dve.tensor_tensor(inter_lo[:, j, :], inter[:, j, :], inter_hi[:, j, :].bitcast(f32), ALU.subtract
                                  ).then_inc(inter_ready, 1)

            steps = [0]

            def step(ins):
                steps[0] += 1
                ins.then_inc(router_step, 1)

            def router_shift(half):
                b4 = slice(4 * half, 4 * half + 4)
                logits = acc[:, 2 + half, 0:4 * LOGITS].rearrange("p (b e) -> p b e", b=4)
                dve.wait_ge(logits_ready, half + 1)
                for b in range(4):
                    step(dve.max(top8[:, 4 * half + b, :], logits[:, b, 0:EXPERTS]))
                step(dve.tensor_scalar(small[:, half, 4 * TOP:4 * TOP + 4], logits[:, :, EXPERTS], -1.0, None,
                                       ALU.mult))
                dve.wait_ge(router_step, steps[0] - 1)
                for b in range(4):
                    step(dve.match_replace(shifted[:, 4 * half + b, 1, :], top8[:, 4 * half + b, :],
                                           logits[:, b, 0:EXPERTS], -3.0e38))
                step(dve.tensor_tensor(small[:, half, 0:4 * TOP].rearrange("p (b e) -> p b e", b=4),
                                       top8[:, b4, :], top8[:, b4, 0:1].to_broadcast([128, 4, TOP]), ALU.subtract))
                step(dve.tensor_tensor(shifted[:, b4, 0, :], logits[:, :, 0:EXPERTS],
                                       top8[:, b4, 0:1].to_broadcast([128, 4, EXPERTS]), ALU.subtract))
                dve.wait_ge(router_step, steps[0])
                dve.tensor_tensor(shifted[:, b4, 1, :], shifted[:, b4, 1, :],
                                  top8[:, b4, 0:1].to_broadcast([128, 4, EXPERTS]), ALU.subtract
                                  ).then_inc(shifted_ready, 1)

            def router_normalise(half):
                b4 = slice(4 * half, 4 * half + 4)
                dve.wait_ge(exp_ready, 2 * half + 1)
                step(dve.tensor_reduce(denom[:, half, 0:4],
                                       small[:, half, 0:4 * TOP].rearrange("p (b e) -> p b e", b=4), AX.X, ALU.add))
                step(dve.tensor_scalar(denom[:, half, 4:8], small[:, half, 4 * TOP:4 * TOP + 4], 1.0, None, ALU.add))
                dve.wait_ge(router_step, steps[0])
                step(dve.reciprocal(recip[:, half, :], denom[:, half, :]))
                dve.wait_ge(exp_ready, 2 * half + 2)
                step(dve.tensor_tensor(route[:, b4, 0:EXPERTS], shifted[:, b4, 0, :], shifted[:, b4, 1, :],
                                       ALU.subtract))
                dve.wait_ge(router_step, steps[0])
                dve.tensor_copy(route[:, b4, EXPERTS], recip[:, half, 4:8]).then_inc(route_ready, 1)
                dve.tensor_tensor(route[:, b4, 0:EXPERTS], route[:, b4, 0:EXPERTS],
                                  recip[:, half, 0:4].rearrange("p (b e) -> p b e", e=1)
                                  .to_broadcast([128, 4, EXPERTS]), ALU.mult).then_inc(route_ready, 1)

            def shared_split_gu():
                dve.wait_ge(sh_gu_hi_ready, 1)
                dve.tensor_tensor(sh_gu_lo[:, :], sh_gu_raw[:, :], sh_gu_hi[:, :].bitcast(f32), ALU.subtract
                                  ).then_inc(sh_gu_ready, 1)

            def shared_split_dp():
                dve.wait_ge(sh_dp_hi_ready, 1)
                dve.tensor_tensor(sh_dp_lo[:, :], sh_dp_raw[:, :], sh_dp_hi[:, :].bitcast(f32), ALU.subtract
                                  ).then_inc(sh_dp_ready, 1)

            def shared_gate(half):
                dve.wait_ge(sh_silu_done, half + 1)
                dve.tensor_tensor(sh_inter[:, half, :], sh_silu[:, half, :], gate_ps[INNER:128, half, :], ALU.mult
                                  ).then_inc(sh_gated, 1)

            def shared_inter_split(half):
                dve.wait_ge(sh_inter_hi_ready, half + 1)
                dve.tensor_tensor(sh_inter_parts[INNER:128, half, :], sh_inter[:, half, :],
                                  sh_inter_parts[0:INNER, half, :].bitcast(f32), ALU.subtract
                                  ).then_inc(sh_inter_ready, 1)

            h_split(0)
            split_gu(0, 0)
            h_split(1)
            split_gu(0, 1)
            shared_split_gu()
            router_shift(0)
            split_dp(0, 0)
            split_dp(0, 1)
            router_normalise(0)
            gate(0, 0, True)
            gate(0, 1, True)
            router_shift(1)
            gate(0, 2, True)
            router_normalise(1)
            split_gu(1, 0)
            gate(0, 3, True)
            shared_gate(0)
            shared_gate(1)
            shared_split_dp()

            def slot(i, j, end=False):
                gate(i, j, False)
                if j == 0:
                    split_gu(i, 1)
                if j == 2 and not end:
                    split_gu(i + 1, 0)
                if j >= LAG:
                    inter_split(i, j - LAG)
                else:
                    inter_split(i - 1, j - LAG + SLOTS)
                if j % 2 == 1:
                    split_dp(i, j // 2)

            inter_split(0, 0)
            for j in range(SLOTS):
                slot(1, j)
            for half in range(2):
                shared_inter_split(half)
            with dve.Fori(2, PAIRS // 2 - 1) as i:
                for j in range(SLOTS):
                    slot(i, j)
            for j in range(SLOTS):
                slot(PAIRS // 2 - 1, j, end=True)
            for j in range(SLOTS - LAG, SLOTS):
                inter_split(PAIRS // 2 - 1, j)
            dve.wait_ge(xt_in, 16)
            for half, k, cols in PIECES:
                dve.wait_ge(acc_done, 2 * half + k + 1)
                in_bank = slice(cols.start - half * HALF, cols.stop - half * HALF)
                dve.tensor_tensor(out_sb[:, k, cols], acc[:, 2 * k + half, in_bank], xt_sb[:, k, cols], ALU.add
                                  ).then_inc(out_ready, 1)

        @block.tensor
        def _(pe):
            def passes(out, w_hi, w_lo, m_hi, m_lo, start, stop):
                pe.matmul(out, w_hi, m_hi, start=start, stop=False)
                pe.matmul(out, w_hi, m_lo, start=False, stop=False)
                return pe.matmul(out, w_lo, m_hi, start=False, stop=stop)

            def condition(half):
                pe.wait_ge(x_in[half], 16)
                pe.wait_ge(diag_ready, 4 * half + 4)
                for k in range(KC):
                    for g in range(GROUPS // 2):
                        gg = half * (GROUPS // 2) + g
                        mm = pe.matmul(acc[:, 2 * k + half, g * 128:g * 128 + 128],
                                       x_sb[:, gg, k * 128:k * 128 + 128], diag[:, gg, :], start=True, stop=True)
                    mm.then_inc(h_ps_ready, 1)

            def logits(half):
                for k in range(KC):
                    pe.wait_ge(h_ready, 2 * half + k + 1)
                    n = slice(half * HALF, (half + 1) * HALF)
                    mm = passes(acc[0:LOGITS, half, :], rw_hi[:, k, :], rw_lo[:, k, :], h_hi[:, k, n], h_lo[:, k, n],
                                k == 0, k == KC - 1)
                mm.then_inc(logit_t_ps_ready, 1)

            def logits_transpose(half):
                pe.wait_ge(logit_t_ready, half + 1)
                for b in range(4):
                    n = slice((4 * half + b) * 128, (4 * half + b + 1) * 128)
                    mm = pe.transpose(acc[:, 2 + half, b * LOGITS:(b + 1) * LOGITS], logit_t[:, n],
                                      ident[0:LOGITS, 0:LOGITS])
                mm.then_inc(logits_ready, 1)

            def route_transpose(half):
                pe.wait_ge(route_ready, 2 * half + 2)
                for b in range(4):
                    mm = pe.transpose(acc[0:EXPERTS + 1, half, b * 128:b * 128 + 128],
                                      route[:, 4 * half + b, :], ident[:, :])
                mm.then_inc(route_t_ps_ready, 1)

            def product(i, j, part, bank, done):
                s, half = j // 2, j % 2
                for k in range(KC):
                    w = slice(k * 256 + part * 128, k * 256 + part * 128 + 128)
                    n = slice(half * HALF, (half + 1) * HALF)
                    mm = passes(bank[:, half, :], gu_hi[:, s, w], gu_lo[:, s, w], h_hi[:, k, n], h_lo[:, k, n],
                                k == 0, k == KC - 1)
                mm.then_inc(done, 1)

            def gate_up(i, j, first):
                if j % 2 == 0:
                    pe.wait_ge(gu_ready, i * 2 + (j // 2 + 1))
                if not (first and j < 2):
                    pe.wait_ge(gated, i * 4 + (j - 1))
                product(i, j, 0, gate_ps, gate_done)
                product(i, j, 1, up_ps, up_done)

            def gate_up_after_shared(j):
                if j == 0:
                    pe.wait_ge(gu_ready, 3)
                pe.wait_ge(gated, SLOTS + j - 1)
                product(1, j, 1, up_ps, up_done)
                pe.wait_ge(sh_gated, j + 1)
                product(1, j, 0, gate_ps, gate_done)

            def shared_gate_up(half):
                pe.wait_ge(gated, half + 3)
                n = slice(half * HALF, (half + 1) * HALF)
                for k in range(KC):
                    w = slice(k * 128, k * 128 + 128)
                    mm = passes(gate_ps[:, half, :], sh_gu_hi[:, w], sh_gu_lo[:, w], h_hi[:, k, n], h_lo[:, k, n],
                                k == 0, k == KC - 1)
                mm.then_inc(sh_gate_up_done, 1)

            def shared_down(half):
                pe.wait_ge(sh_inter_ready, half + 1)
                for k in range(KC):
                    w, out = slice(k * 128, k * 128 + 128), acc[:, 2 * k + half, :]
                    pe.matmul(out, sh_dp_hi[:, w], sh_inter_parts[:, half, :], start=False, stop=False)
                    pe.matmul(out, sh_dp_lo[0:INNER, w], sh_inter_parts[0:INNER, half, :], start=False, stop=False)

            def down(i, j, first):
                s, half = j // 2, j % 2
                if half == 0:
                    pe.wait_ge(dp_ready, i * 2 + (s + 1))
                pe.wait_ge(inter_ready, i * 4 + (j + 1))
                for k in range(KC):
                    w = slice(k * 128, k * 128 + 128)
                    mm = passes(acc[:, 2 * k + half, :], dp_hi[:, s, w], dp_lo[:, s, w],
                                inter_hi[:, j, :], inter_lo[:, j, :], first and s == 0, False)
                mm.then_inc(down_done, 1)

            def last_down(half, order):
                for s, k in order:
                    w = slice(k * 128, k * 128 + 128)
                    pe.wait_ge(dp_ready, PAIRS - 1 + s)
                    pe.wait_ge(inter_ready, UNITS - 3 + 2 * s + half)
                    mm = passes(acc[:, 2 * k + half, :], dp_hi[:, s, w], dp_lo[:, s, w],
                                inter_hi[:, 2 * s + half, :], inter_lo[:, 2 * s + half, :], False, s == 1)
                    if s == 1:
                        mm.then_inc(acc_done, 1)

            pe.wait_ge(ident_step, 2)
            with pe.Fori(0, WARM_UP // 4) as _:
                for _ in range(4):
                    pe.matmul(gate_ps[:, 0, 0:128], ident[:, :], ident[:, :], start=True, stop=True)
            condition(0)
            condition(1)
            pe.wait_ge(rw_ready, 1)
            logits(0)
            logits(1)
            logits_transpose(0)
            pe.wait_ge(gu_ready, 1)
            product(0, 0, 0, gate_ps, gate_done)
            logits_transpose(1)
            product(0, 0, 1, up_ps, up_done)
            gate_up(0, 1, True)
            route_transpose(0)
            gate_up(0, 2, True)
            gate_up(0, 3, True)
            pe.wait_ge(sh_gu_ready, 1)
            route_transpose(1)
            shared_gate_up(0)
            shared_gate_up(1)
            for j in range(SLOTS):
                if j < 2:
                    gate_up_after_shared(j)
                else:
                    gate_up(1, j, False)
                down(0, j, True)
            with pe.Fori(2, PAIRS // 2) as i:
                for j in range(SLOTS):
                    gate_up(i, j, False)
                    down(i - 1, j, False)
            pe.wait_ge(sh_dp_ready, 1)
            for half in range(2):
                shared_down(half)
            last_down(0, [(s, k) for s in range(2) for k in range(KC)])
            last_down(1, [(s, k) for k in range(KC) for s in range(2)])


def kernel(x, itok_B_1_198, L0_cond_weights, L0_ffn_gate_w, L0_ffn_gu_w, L0_ffn_dp_w, L0_ffn_sh_gate_w,
           L0_ffn_sh_up_w, L0_ffn_sh_down_w, L0_ffn_sh_gate1_w):
    import numpy as np
    import concourse.bacc as bacc
    from concourse.bass_utils import run_bass_kernel_spmd

    x, gu, dp = np.asarray(x), np.asarray(L0_ffn_gu_w), np.asarray(L0_ffn_dp_w)
    sh_gate, sh_up, sh_down = map(np.asarray, (L0_ffn_sh_gate_w, L0_ffn_sh_up_w, L0_ffn_sh_down_w))
    f32 = gu.dtype

    gu_all = gu.reshape(PAIRS, 2, 2, INNER, KC, 128).transpose(0, 5, 4, 2, 1, 3).reshape(
        PAIRS, 128, KC * 256)
    sh_gu = np.stack([w.reshape(INNER, KC, 128).transpose(2, 1, 0) for w in (sh_gate, sh_up)], axis=2)
    dp_all = dp.reshape(PAIRS, 2, TIME, INNER).transpose(0, 1, 3, 2).reshape(PAIRS, 128, TIME)
    router = np.zeros((TIME, LOGITS), f32)
    router[:, :EXPERTS] = np.asarray(L0_ffn_gate_w).T
    router[:, EXPERTS] = np.asarray(L0_ffn_sh_gate1_w)[0]

    arrays = {
        "x": np.ascontiguousarray(x.reshape(BATCH * CHAN, TIME)),
        "x_t": np.ascontiguousarray(x.reshape(TOKENS, TIME).T),
        "itok": np.ascontiguousarray(itok_B_1_198).reshape(BATCH, 1),
        "cond_w": np.ascontiguousarray(np.asarray(L0_cond_weights).reshape(STATES, CHAN * COND)),
        "router_w": router,
        "gu_w": np.ascontiguousarray(gu_all),
        "dp_w": np.ascontiguousarray(dp_all),
        "sh_gu_w": np.ascontiguousarray(sh_gu).reshape(128, KC * 128),
        "sh_dp_w": np.concatenate([sh_down.T, sh_down.T]),
    }
    nc = bacc.Bacc("TRN2", target_bir_lowering=False, num_devices=1)
    args = [nc.dram_tensor(f"in_{n}", a.shape, mybir.dt.from_np(a.dtype), kind="ExternalInput").ap()
            for n, a in arrays.items()]
    out = nc.dram_tensor("out_t", (TIME, TOKENS), mybir.dt.from_np(x.dtype), kind="ExternalOutput").ap()
    adaln_moe_kernel(nc, *args, out)
    r = run_bass_kernel_spmd(nc, [{f"in_{n}": a for n, a in arrays.items()}], core_ids=[0])
    return np.ascontiguousarray(r.results[0]["out_t"].T).reshape(x.shape)
```
